# Optimizing a Trainium2 kernel written in Bass

```python
import numpy as np
import jax
import jax.numpy as jnp

def _softmax(x, axis=-1):
    return jax.nn.softmax(x, axis=axis)

def _gelu(x):
    return jax.nn.gelu(x, approximate=True)

def _silu(x):
    return jax.nn.silu(x)

def _sigmoid(x):
    return jax.nn.sigmoid(x)

def _layernorm(x, axis=-1, eps=1e-05):
    m = jnp.mean(x, axis=axis, keepdims=True)
    v = jnp.var(x, axis=axis, keepdims=True)
    return (x - m) / jnp.sqrt(v + eps)

def _scatter_add(tgt, idx, src, axis=0):
    return tgt.at[idx].add(src)

def _segment_sum(src, seg, n):
    return jax.ops.segment_sum(src, seg, n)
kernel_name = 'mk_rec_standalone_d1_rec_r8_655b7a'

def setup_inputs(seed: int=0):
    np.random.seed(seed)
    _w = jnp.asarray

    def _rec_inputs():
        import jax
        import jax.numpy as jnp
        _rk = jax.random.key(seed)
        r_x = jax.random.randint(jax.random.fold_in(_rk, 1), (2048, 24), 0, 1000, jnp.int32)
        return r_x
    r_x = _rec_inputs()

    def _L0_rec_setup():
        import jax, jax.numpy as jnp
        import numpy as np
        FIELD_DIMS = [1000] * 24
        OFFSETS = np.concatenate([[0], np.cumsum(FIELD_DIMS)[:-1]]).astype(np.int64)
        NUM_FIELDS = len(FIELD_DIMS)
        EMBED_DIM = 128
        N_ATT_LAYERS = 3
        N_HEADS = 2
        key = jax.random.key(seed)
        ks = jax.random.split(key, 10)
        B = 2048
        F, E = (NUM_FIELDS, EMBED_DIM)
        D = F * E
        x = jax.random.randint(ks[0], (B, F), 0, 1000, dtype=jnp.int64)
        emb_table = jax.random.normal(ks[1], (sum(FIELD_DIMS), E), jnp.float32) * 0.05
        Wq = jax.random.normal(ks[2], (N_ATT_LAYERS, E, E), jnp.float32) * (1.0 / np.sqrt(E))
        Wk = jax.random.normal(ks[3], (N_ATT_LAYERS, E, E), jnp.float32) * (1.0 / np.sqrt(E))
        Wv = jax.random.normal(ks[4], (N_ATT_LAYERS, E, E), jnp.float32) * (1.0 / np.sqrt(E))
        final_w = jax.random.normal(ks[5], (D, 1), jnp.float32) * 0.0001
        W1 = jax.random.normal(ks[6], (D, 32), jnp.float32) * (1.0 / np.sqrt(D))
        b1 = jnp.zeros((32,), jnp.float32)
        W2 = jax.random.normal(ks[7], (32, 32), jnp.float32) * (1.0 / np.sqrt(32))
        b2 = jnp.zeros((32,), jnp.float32)
        W3 = jax.random.normal(ks[8], (32, 1), jnp.float32) * (1.0 / np.sqrt(32))
        b3 = jnp.zeros((1,), jnp.float32)
        return dict(x=x, emb_table=emb_table, Wq=Wq, Wk=Wk, Wv=Wv, final_w=final_w, W1=W1, b1=b1, W2=W2, b2=b2, W3=W3, b3=b3)
    _L0_rec_all = _L0_rec_setup()
    _L0_rec_in = {k: v for k, v in _L0_rec_all.items() if k in ('emb_table', 'Wq', 'Wk', 'Wv', 'final_w', 'W1', 'b1', 'W2', 'b2', 'W3', 'b3')}
    del _L0_rec_all
    return {'r_x': r_x, 'L0_rec_emb_table': _L0_rec_in['emb_table'], 'L0_rec_Wq': _L0_rec_in['Wq'], 'L0_rec_Wk': _L0_rec_in['Wk'], 'L0_rec_Wv': _L0_rec_in['Wv'], 'L0_rec_final_w': _L0_rec_in['final_w'], 'L0_rec_W1': _L0_rec_in['W1'], 'L0_rec_b1': _L0_rec_in['b1'], 'L0_rec_W2': _L0_rec_in['W2'], 'L0_rec_b2': _L0_rec_in['b2'], 'L0_rec_W3': _L0_rec_in['W3'], 'L0_rec_b3': _L0_rec_in['b3']}

def reference(r_x, L0_rec_emb_table, L0_rec_Wq, L0_rec_Wk, L0_rec_Wv, L0_rec_final_w, L0_rec_W1, L0_rec_b1, L0_rec_W2, L0_rec_b2, L0_rec_W3, L0_rec_b3):
    import jax
    import jax.numpy as jnp

    def _L0_rec_ref(x, emb_table, Wq, Wk, Wv, final_w, W1, b1, W2, b2, W3, b3):
        import jax, jax.numpy as jnp
        import numpy as np
        FIELD_DIMS = [1000] * 24
        OFFSETS = np.concatenate([[0], np.cumsum(FIELD_DIMS)[:-1]]).astype(np.int64)
        NUM_FIELDS = len(FIELD_DIMS)
        EMBED_DIM = 128
        N_ATT_LAYERS = 3
        N_HEADS = 2
        B, F = x.shape
        E, H = (EMBED_DIM, N_HEADS)
        dh = E // H
        ids = x + jnp.asarray(OFFSETS)
        e = emb_table[ids]
        att = e
        for l in range(N_ATT_LAYERS):
            Q = (att @ Wq[l]).reshape(B, F, H, dh)
            K = (att @ Wk[l]).reshape(B, F, H, dh)
            V = (att @ Wv[l]).reshape(B, F, H, dh)
            scores = jnp.einsum('bfhd,bghd->bhfg', Q, K)
            probs = jax.nn.softmax(scores, axis=-1)
            out = jnp.einsum('bhfg,bghd->bfhd', probs, V).reshape(B, F, E)
            att = out + att
        att_out = att.reshape(B, F * E) @ final_w
        d = e.reshape(B, F * E)
        h = jax.nn.relu(d @ W1 + b1)
        h = jax.nn.relu(h @ W2 + b2)
        dnn_out = jax.nn.sigmoid(h @ W3 + b3)
        return jax.nn.sigmoid(att_out + dnn_out)
    y = _L0_rec_ref(r_x, L0_rec_emb_table, L0_rec_Wq, L0_rec_Wk, L0_rec_Wv, L0_rec_final_w, L0_rec_W1, L0_rec_b1, L0_rec_W2, L0_rec_b2, L0_rec_W3, L0_rec_b3)
    return y

_drawn_inputs = setup_inputs


def setup_inputs(seed=0):
    import zlib

    import numpy as np

    out = dict(_drawn_inputs(seed))
    spreads = {'L0_rec_b1': (0.0, 0.8), 'L0_rec_b2': (0.0, 0.8)}
    factors = {'L0_rec_emb_table': 8.0,
     'L0_rec_Wq': 8.0,
     'L0_rec_Wk': 8.0,
     'L0_rec_Wv': 8.0,
     'L0_rec_final_w': 8.0,
     'L0_rec_W1': 8.0,
     'L0_rec_W2': 8.0,
     'L0_rec_W3': 8.0}
    for name, (base, spread) in spreads.items():
        noise = np.random.default_rng([zlib.crc32(name.encode()), seed]).standard_normal(out[name].shape)
        drawn = base * np.exp(spread * noise) if base else spread * noise
        out[name] = jnp.asarray(drawn.astype(out[name].dtype))
    for name, factor in factors.items():
        out[name] = (out[name] * factor).astype(out[name].dtype)
    return out
```

```python
import concourse.bass as bass
from concourse import mybir
from contextlib import ExitStack


def attention_recommender_kernel(
    nc: bass.Bass,
    x: bass.AP,
    emb_table: bass.AP,
    Wq: bass.AP,
    Wk: bass.AP,
    Wv: bass.AP,
    final_w: bass.AP,
    W1: bass.AP,
    b1: bass.AP,
    W2: bass.AP,
    b2: bass.AP,
    W3: bass.AP,
    b3: bass.AP,
    consts: bass.AP,
    out: bass.AP,
):
    fp32 = mybir.dt.float32
    i32 = mybir.dt.int32
    ALU = mybir.AluOpType
    ACT = mybir.ActivationFunctionType
    AX = mybir.AxisListType

    B, F = x.shape
    E = emb_table.shape[1]
    L = Wq.shape[0]
    HID = W1.shape[1]
    H = 2
    DH = E // H
    P = 128
    Q = 32
    QB = P // Q
    SB = 16
    T = SB // QB
    NS = 4
    ITB = NS * SB
    NI = B // ITB
    JOBS = L * NS
    LAST = NI - 1
    ROWS = SB * F
    GPS = ROWS // P
    NG = B * F // P
    PREP = JOBS - NS
    DNN0 = 4
    DNN_SLOTS = 3
    FM = F // QB
    CH = 512

    x_rows = x.rearrange("b f -> (b f)").rearrange("(c n p) -> n c p", c=NG // P, p=P)
    w1_v = W1.rearrange("(f e) h -> e f h", f=F)
    fw_v = final_w.rearrange("(f e) o -> f (e o)", f=F)

    ctx = ExitStack()
    with ctx:
        def sb(name, shape, dt=fp32):
            return ctx.enter_context(nc.sbuf_tensor(name, shape, dt))

        def pb(name, shape):
            return ctx.enter_context(nc.psum_tensor(name, shape, fp32))

        def sem(name):
            return ctx.enter_context(nc.semaphore(name))

        cst = sb("cst", [P, P + HID + 3])
        ident = cst[:, 0:P]
        fold = cst[:, P:P + HID]
        field_base = cst[:, P + HID:P + HID + 3]
        wq_sb = sb("wq_sb", [P, L, E])
        wk_sb = sb("wk_sb", [P, L, E])
        wv_sb = sb("wv_sb", [P, L, E])
        wqT = sb("wqT", [P, L, E])
        wkT = sb("wkT", [P, L, E])
        mT = sb("mT", [P, L, H, E])
        w1_sb = sb("w1_sb", [P, F, HID])
        fw_rows = sb("fw_rows", [F, E])
        fwT = sb("fwT", [P, F])
        b1_sb = sb("b1_sb", [HID, 1])
        b2_sb = sb("b2_sb", [HID, 1])
        b3_sb = sb("b3_sb", [1, 1])
        w2_sb = sb("w2_sb", [HID, HID])
        w3_sb = sb("w3_sb", [HID, 1])
        ones = sb("ones", [P, 1])
        x_int = sb("x_int", [P, NG // P, P], i32)
        x_f = sb("x_f", [P, NG // P, P])
        ids = sb("ids", [P, NG], i32)
        ids_now = sb("ids_now", [P, NS * GPS], i32)
        rows = sb("rows", [P, NS * GPS, E])
        eT = sb("eT", [P, NS, SB, Q])
        attT = sb("attT", [P, NS, SB, Q])
        keys = sb("keys", [P, H, SB, F])
        values = sb("values", [P, 3, T, E])
        centred = sb("centred", [P, 2, T * H, F])
        probs = sb("probs", [P, 2, T * H, Q])
        probsT = sb("probsT", [P, 2, T * H, Q])
        blocks = sb("blocks", [P, 3, T * H, QB, F])
        row_max = sb("row_max", [P, T * H])
        row_sum = sb("row_sum", [P, T * H])
        row_inv = sb("row_inv", [P, T * H])
        weighted = sb("weighted", [P, SB, F])
        att_part = sb("att_part", [P, B])
        h1_part = sb("h1_part", [P, B])
        h1 = sb("h1", [HID, B])
        h2 = sb("h2", [HID, B])
        dnn = sb("dnn", [1, B])
        logit = sb("logit", [1, B])
        y = sb("y", [1, B])

        keys_ps = pb("keys_ps", [P, H, 512])
        values_ps = pb("values_ps", [P, T, E])
        scores_ps = pb("scores_ps", [P, 2, 512])
        out_ps = pb("out_ps", [P, 512])
        turn_ps = pb("turn_ps", [P, 512])
        dnn_ps = pb("dnn_ps", [P, 512])

        loaded = sem("loaded")
        x_loaded = sem("x_loaded")
        cst_loaded = sem("cst_loaded")
        zeroed = sem("zeroed")
        x_float = sem("x_float")
        x_turned = sem("x_turned")
        ids_ready = sem("ids_ready")
        w_turned = sem("w_turned")
        w_copied = sem("w_copied")
        m_done = sem("m_done")
        m_copied = sem("m_copied")
        ids_copied = sem("ids_copied")
        gathered = [sem(f"gathered{s}") for s in range(NS)]
        rows_turned = sem("rows_turned")
        rows_free = sem("rows_free")
        e_copied = sem("e_copied")
        keys_done = sem("keys_done")
        keys_copied = sem("keys_copied")
        values_done = sem("values_done")
        values_copied = sem("values_copied")
        scores_done = sem("scores_done")
        maxed = sem("maxed")
        centred_done = sem("centred_done")
        exp_done = sem("exp_done")
        summed = sem("summed")
        inverted = sem("inverted")
        normed = sem("normed")
        probs_turned = sem("probs_turned")
        blocks_done = sem("blocks_done")
        out_done = sem("out_done")
        att_done = sem("att_done")
        weighted_done = sem("weighted_done")
        part_done = sem("part_done")
        dnn_done = sem("dnn_done")
        dnn_copied = sem("dnn_copied")
        tail_pe = sem("tail_pe")
        h1_done = sem("h1_done")
        h2_done = sem("h2_done")
        sig_done = sem("sig_done")
        logit_done = sem("logit_done")
        y_done = sem("y_done")
        stored = sem("stored")

        N_ZEROED = 6
        block = ctx.enter_context(nc.Block())

        @block.sync
        def _(sp):
            sp.dma_start(x_int[:], x_rows).then_inc(x_loaded, 16)
            sp.dma_start(cst[:], consts).then_inc(cst_loaded, 16)
            sp.dma_start(wq_sb[:], Wq.rearrange("l e n -> e l n")).then_inc(loaded, 16)
            sp.dma_start(wk_sb[:], Wk.rearrange("l e n -> e l n")).then_inc(loaded, 16)
            sp.dma_start(fw_rows[:], fw_v).then_inc(loaded, 16)
            sp.dma_start(wv_sb[:], Wv.rearrange("l e n -> e l n")).then_inc(loaded, 16)
            sp.dma_start(w1_sb[:], w1_v).then_inc(loaded, 16)
            sp.dma_start(w2_sb[:], W2).then_inc(loaded, 16)
            sp.dma_start(w3_sb[:], W3).then_inc(loaded, 16)
            sp.dma_start(b1_sb[:], b1[:, None]).then_inc(loaded, 16)
            sp.dma_start(b2_sb[:], b2[:, None]).then_inc(loaded, 16)
            sp.dma_start(b3_sb[:], b3[:, None]).then_inc(loaded, 16)
            sp.wait_ge(y_done, B // CH)
            sp.dma_start(out.rearrange("b o -> o b"), y[:]).then_inc(stored, 16)
            sp.wait_ge(stored, 16)

        N_LOADED = 16 * 10

        @block.gpsimd
        def _(pool):
            def gather_iteration(i, first):
                if not first:
                    pool.wait_ge(gathered[NS - 1], 16 * GPS * i)
                nc.gpsimd.tensor_copy(ids_now[:], ids[:, bass.ds(i * (NS * GPS), NS * GPS)]).then_inc(ids_copied, 1)
                pool.wait_ge(ids_copied, i + 1)
                for s in range(NS):
                    if not first:
                        pool.wait_ge(rows_turned, (i - 1) * NS + s + 1)
                        pool.sem_inc(rows_free, 1)
                    for k in range(GPS):
                        nc.gpsimd.indirect_dma_start(
                            out=rows[:, s * GPS + k, :], out_offset=None, in_=emb_table,
                            in_offset=bass.IndirectOffsetOnAxis(ap=ids_now[:, s * GPS + k:s * GPS + k + 1], axis=0),
                        ).then_inc(gathered[s], 16)

            nc.gpsimd.memset(blocks[:], 0.0).then_inc(zeroed, 1)
            nc.gpsimd.memset(ones[:], 1.0).then_inc(zeroed, 1)
            pool.wait_ge(ids_ready, NG // P)
            gather_iteration(0, True)
            with pool.Fori(1, NI) as i:
                gather_iteration(i, False)

        @block.tensor
        def _(pe):
            def turn_rows(i, s):
                n = i * NS + s
                pe.wait_ge(gathered[s], (i + 1) * (16 * GPS))
                pe.wait_ge(e_copied, n + 1)
                for k in range(GPS):
                    last = nc.tensor.transpose(turn_ps[:, k * P:(k + 1) * P], rows[:, s * GPS + k, :], ident)
                last.then_inc(rows_turned, 1)

            def slot(i, c, first=False, drain=False):
                k = i * JOBS + c
                if not (first and c < 1) and c - 1 < JOBS:
                    b = (c - 1) % JOBS
                    src = eT if b < NS else attT
                    st = b % NS
                    pe.wait_ge(keys_copied, k)
                    if not (first and c < 3):
                        pe.wait_ge(centred_done, k - 2)
                    for m in range(SB):
                        q, t = m % QB, m // QB
                        last = nc.tensor.matmul(
                            scores_ps[q * Q:(q + 1) * Q, b % 2, t * H * F:(t + 1) * H * F].rearrange(
                                "p (h g) -> p h g", h=H),
                            src[:, st, m, :], keys[:, :, m, :], start=True, stop=True)
                    last.then_inc(scores_done, 1)
                if not drain:
                    lay, st = c // NS, c % NS
                    src = eT if lay == 0 else attT
                    if lay == 0:
                        pe.wait_ge(e_copied, i * NS + st + 2)
                    else:
                        pe.wait_ge(att_done, k - NS + 1)
                    for h in range(H):
                        last = nc.tensor.matmul(
                            keys_ps[:, h, 0:ROWS].rearrange("p (b f) -> p b f", b=SB),
                            mT[:, lay, h, :], src[:, st, :, 0:F], start=True, stop=True)
                    last.then_inc(keys_done, 1)
                if not (first and c < 3):
                    b = (c - 3) % JOBS
                    pe.wait_ge(blocks_done, k - 2)
                    pe.wait_ge(values_copied, k - 2)
                    if not (first and c < 4):
                        pe.wait_ge(att_done, k - 3)
                    for t in range(T):
                        for h in range(H):
                            last = nc.tensor.matmul(
                                out_ps[h * DH:(h + 1) * DH, t * QB * F:(t + 1) * QB * F],
                                values[:, b % 3, t, h * DH:(h + 1) * DH],
                                blocks[:, b % 3, t * H + h, :, :], start=True, stop=True)
                    last.then_inc(out_done, 1)
                if not drain:
                    if not (first and c < 1):
                        pe.wait_ge(values_copied, k)
                    for t in range(T):
                        last = nc.tensor.matmul(
                            values_ps[:, t, :], src[:, st, t * QB:(t + 1) * QB, :].rearrange("p b f -> p (b f)"),
                            wv_sb[:, lay, :], start=True, stop=True)
                    last.then_inc(values_done, 1)
                if not drain and DNN0 <= c < DNN0 + DNN_SLOTS:
                    if c == DNN0 and not first:
                        pe.wait_ge(dnn_copied, i)
                    step = FM // DNN_SLOTS
                    for m in range((c - DNN0) * step, (c - DNN0 + 1) * step):
                        for q in range(QB):
                            f = m * QB + q
                            last = nc.tensor.matmul(
                                dnn_ps[q * Q:(q + 1) * Q, 0:ITB], w1_sb[:, f, :],
                                eT[:, :, :, f], start=(m == 0), stop=(m == FM - 1))
                    if c == DNN0 + DNN_SLOTS - 1:
                        last.then_inc(dnn_done, 1)

            pe.wait_ge(cst_loaded, 16)
            for c in range(NG // P):
                pe.wait_ge(x_float, c + 1)
                if c:
                    pe.wait_ge(ids_ready, c)
                nc.tensor.transpose(turn_ps[:, 0:P], x_f[:, c, :], ident).then_inc(x_turned, 1)
            pe.wait_ge(loaded, N_LOADED)
            for lay in range(L):
                if lay:
                    pe.wait_ge(w_copied, lay)
                nc.tensor.transpose(out_ps[:, 0:P], wq_sb[:, lay, :], ident)
                nc.tensor.transpose(out_ps[:, P:2 * P], wk_sb[:, lay, :], ident).then_inc(w_turned, 1)
                pe.wait_ge(w_copied, lay + 1)
                if lay:
                    pe.wait_ge(m_copied, lay)
                for h in range(H):
                    last = nc.tensor.matmul(keys_ps[:, h, 0:E], wkT[h * DH:(h + 1) * DH, lay, :],
                                            wqT[h * DH:(h + 1) * DH, lay, :], start=True, stop=True)
                last.then_inc(m_done, 1)
            pe.wait_ge(ids_ready, NG // P)
            nc.tensor.transpose(turn_ps[:, 0:F], fw_rows[:, :], ident[0:F, 0:F]).then_inc(m_done, 1)
            pe.wait_ge(m_copied, L)
            pe.wait_ge(zeroed, N_ZEROED)
            for s in range(NS):
                turn_rows(0, s)
            for c in range(JOBS):
                slot(0, c, first=True)
                if c >= PREP:
                    turn_rows(1, c - PREP)
            with pe.Fori(1, LAST) as i:
                for c in range(JOBS):
                    slot(i, c)
                    if c >= PREP:
                        turn_rows(i + 1, c - PREP)
            for c in range(JOBS):
                slot(LAST, c)
            for c in range(JOBS, JOBS + 3):
                slot(LAST, c, drain=True)

            pe.wait_ge(dnn_copied, NI)
            pe.wait_ge(part_done, NI * NS)
            for c in range(B // CH):
                col = slice(c * CH, (c + 1) * CH)
                if c:
                    pe.wait_ge(y_done, c)
                nc.tensor.matmul(keys_ps[0:HID, 0, :], fold, h1_part[:, col], start=True, stop=True)
                nc.tensor.matmul(out_ps[0:1, :], ones[:], att_part[:, col], start=True, stop=True).then_inc(tail_pe, 1)
                pe.wait_ge(h1_done, c + 1)
                nc.tensor.matmul(keys_ps[0:HID, 1, :], w2_sb[:], h1[:, col], start=True, stop=True).then_inc(tail_pe, 1)
                pe.wait_ge(h2_done, c + 1)
                nc.tensor.matmul(turn_ps[0:1, :], w3_sb[:], h2[:, col], start=True, stop=True).then_inc(tail_pe, 1)

        @block.scalar
        def _(act):
            def copy_rows(i, s, first):
                act.wait_ge(rows_turned, i * NS + s + 1)
                if not first:
                    act.wait_ge(dnn_done, i)
                    act.wait_ge(att_done, (i - 1) * JOBS + s + 1)
                nc.scalar.copy(eT[:, s, :, 0:F],
                               turn_ps[:, 0:ROWS].rearrange("p (b f) -> p b f", b=SB)).then_inc(e_copied, 1)

            def slot(i, c, first=False, drain=False):
                k = i * JOBS + c
                if not (first and c < 1) and c - 1 < JOBS:
                    b = (c - 1) % JOBS
                    act.wait_ge(values_done, k)
                    if not (first and c < 4):
                        act.wait_ge(out_done, k - 3)
                    nc.scalar.copy(values[:, b % 3, :, :], values_ps[:, :, :]).then_inc(values_copied, 1)
                if not (first and c < 2) and c - 2 < JOBS:
                    b = (c - 2) % JOBS
                    act.wait_ge(probs_turned, k - 1)
                    if not (first and c < 5):
                        act.wait_ge(out_done, k - 4)
                    for q in range(QB):
                        p = slice(q * Q, (q + 1) * Q)
                        last = nc.scalar.copy(blocks[p, b % 3, :, q, :], probsT[p, b % 2, :, 0:F])
                    last.then_inc(blocks_done, 1)
                if not (first and c < 1) and c - 1 < JOBS:
                    b = (c - 1) % JOBS
                    act.wait_ge(centred_done, k)
                    if not (first and c < 3):
                        act.wait_ge(probs_turned, k - 2)
                    nc.scalar.activation(probs[:, b % 2, :, 0:F], centred[:, b % 2, :, :],
                                         ACT.Exp).then_inc(exp_done, 1)
                if not drain:
                    act.wait_ge(keys_done, k + 1)
                    if not (first and c < 1):
                        act.wait_ge(scores_done, k)
                    nc.scalar.copy(keys[:].rearrange("p h b f -> p h (b f)"), keys_ps[:, :, 0:ROWS]).then_inc(keys_copied, 1)
                if not drain and c == DNN0 + DNN_SLOTS:
                    act.wait_ge(dnn_done, i + 1)
                    nc.scalar.copy(h1_part[:, bass.ds(i * ITB, ITB)], dnn_ps[:, 0:ITB]).then_inc(dnn_copied, 1)

            for lay in range(L):
                act.wait_ge(w_turned, lay + 1)
                nc.scalar.copy(wqT[:, lay, :], out_ps[:, 0:P])
                nc.scalar.copy(wkT[:, lay, :], out_ps[:, P:2 * P]).then_inc(w_copied, 1)
                act.wait_ge(m_done, lay + 1)
                nc.scalar.copy(mT[:, lay, :, :], keys_ps[:, :, 0:E]).then_inc(m_copied, 1)
            act.wait_ge(m_done, L + 1)
            nc.scalar.copy(fwT[:], turn_ps[:, 0:F]).then_inc(e_copied, 1)
            act.wait_ge(zeroed, N_ZEROED)
            for s in range(NS):
                copy_rows(0, s, True)
            for c in range(JOBS):
                slot(0, c, first=True)
                if c >= PREP:
                    copy_rows(1, c - PREP, False)
            with act.Fori(1, LAST) as i:
                for c in range(JOBS):
                    slot(i, c)
                    if c >= PREP:
                        copy_rows(i + 1, c - PREP, False)
            for c in range(JOBS):
                slot(LAST, c)
            for c in range(JOBS, JOBS + 3):
                slot(LAST, c, drain=True)

            for c in range(B // CH):
                col = slice(c * CH, (c + 1) * CH)
                act.wait_ge(tail_pe, 3 * c + 1)
                nc.scalar.activation(h1[:, col], keys_ps[0:HID, 0, :], ACT.Relu, bias=b1_sb[:]).then_inc(h1_done, 1)
                act.wait_ge(tail_pe, 3 * c + 2)
                nc.scalar.activation(h2[:, col], keys_ps[0:HID, 1, :], ACT.Relu, bias=b2_sb[:]).then_inc(h2_done, 1)
                act.wait_ge(tail_pe, 3 * c + 3)
                nc.scalar.activation(dnn[:, col], turn_ps[0:1, :], ACT.Sigmoid, bias=b3_sb[:]).then_inc(sig_done, 1)
                act.wait_ge(logit_done, c + 1)
                nc.scalar.activation(y[:, col], logit[:, col], ACT.Sigmoid).then_inc(y_done, 1)

        @block.vector
        def _(dve):
            def slot(i, c, first=False):
                k = i * JOBS + c
                if not (first and c < 1) and c - 1 < JOBS:
                    b = (c - 1) % JOBS
                    sc = scores_ps[:, b % 2, 0:T * H * F].rearrange("p (a g) -> p a g", g=F)
                    dve.wait_ge(scores_done, k)
                    nc.vector.reduce_max(row_max[:], sc, axis=AX.X).then_inc(maxed, 1)
                    dve.wait_ge(maxed, k)
                    if not (first and c < 3):
                        dve.wait_ge(exp_done, k - 2)
                    nc.vector.tensor_tensor(centred[:, b % 2, :, :], sc,
                                            row_max[:].unsqueeze(2).to_broadcast([P, T * H, F]),
                                            ALU.subtract).then_inc(centred_done, 1)
                    dve.wait_ge(exp_done, k)
                    nc.vector.reduce_sum(row_sum[:], probs[:, b % 2, :, 0:F], axis=AX.X).then_inc(summed, 1)
                    dve.wait_ge(summed, k)
                    nc.vector.reciprocal(row_inv[:], row_sum[:]).then_inc(inverted, 1)
                    dve.wait_ge(inverted, k)
                    nc.vector.tensor_tensor(probs[:, b % 2, :, 0:F], probs[:, b % 2, :, 0:F],
                                            row_inv[:].unsqueeze(2).to_broadcast([P, T * H, F]),
                                            ALU.mult).then_inc(normed, 1)
                    dve.wait_ge(normed, k)
                    if not (first and c < 3):
                        dve.wait_ge(blocks_done, k - 2)
                    nc.vector.transpose(probsT[:, b % 2, :, :].rearrange("p a g -> p (a g)"),
                                        probs[:, b % 2, :, :].rearrange("p a g -> p (a g)")).then_inc(probs_turned, 1)
                if not (first and c < 3):
                    b = (c - 3) % JOBS
                    lay, st = b // NS, b % NS
                    src = eT if lay == 0 else attT
                    dve.wait_ge(out_done, k - 2)
                    nc.vector.tensor_tensor(attT[:, st, :, 0:F],
                                            out_ps[:, 0:ROWS].rearrange("p (b f) -> p b f", b=SB),
                                            src[:, st, :, 0:F], ALU.add).then_inc(att_done, 1)
                    if lay == L - 1:
                        n = (i if c >= 3 else i - 1) * NS + st
                        dve.wait_ge(att_done, k - 2)
                        nc.vector.tensor_tensor(weighted[:], attT[:, st, :, 0:F],
                                                fwT[:].unsqueeze(1).to_broadcast([P, SB, F]),
                                                ALU.mult).then_inc(weighted_done, 1)
                        dve.wait_ge(weighted_done, n + 1)
                        nc.vector.reduce_sum(att_part[:, bass.ds(n * SB, SB)], weighted[:], axis=AX.X).then_inc(part_done, 1)

            nc.vector.memset(eT[:], 0.0).then_inc(zeroed, 1)
            nc.vector.memset(attT[:], 0.0).then_inc(zeroed, 1)
            nc.vector.memset(probs[:], 0.0).then_inc(zeroed, 1)
            nc.vector.memset(probsT[:], 0.0).then_inc(zeroed, 1)
            dve.wait_ge(x_loaded, 16)
            for c in range(NG // P):
                nc.vector.tensor_copy(x_f[:, c, :], x_int[:, c, :]).then_inc(x_float, 1)
            dve.wait_ge(cst_loaded, 16)
            for c in range(NG // P):
                dve.wait_ge(x_turned, c + 1)
                for r in range(3):
                    first_col = (r - c * P) % 3
                    last = nc.vector.tensor_scalar(ids[:, c * P + first_col:(c + 1) * P:3],
                                                   turn_ps[:, first_col:P:3],
                                                   field_base[:, r:r + 1], None, ALU.add)
                last.then_inc(ids_ready, 1)
            dve.wait_ge(zeroed, N_ZEROED)
            dve.wait_ge(e_copied, 1)
            for c in range(JOBS):
                slot(0, c, first=True)
            with dve.Fori(1, LAST) as i:
                for c in range(JOBS):
                    slot(i, c)
            for c in range(JOBS + 3):
                slot(LAST, c)

            for c in range(B // CH):
                col = slice(c * CH, (c + 1) * CH)
                dve.wait_ge(sig_done, c + 1)
                nc.vector.tensor_tensor(logit[:, col], out_ps[0:1, :], dnn[:, col], ALU.add).then_inc(logit_done, 1)


_INS = ['r_x', 'L0_rec_emb_table', 'L0_rec_Wq', 'L0_rec_Wk', 'L0_rec_Wv', 'L0_rec_final_w', 'L0_rec_W1',
        'L0_rec_b1', 'L0_rec_W2', 'L0_rec_b2', 'L0_rec_W3', 'L0_rec_b3']


def _constants(np):
    P, HID, F, DIM = 128, 32, 24, 1000
    ident = np.eye(P, dtype=np.float32)
    fold = np.tile(np.eye(HID, dtype=np.float32), (P // HID, 1))
    p = np.arange(P)
    base = np.stack([((P * n + p) % F) * DIM for n in range(3)], axis=1).astype(np.float32)
    return np.ascontiguousarray(np.concatenate([ident, fold, base], axis=1))


def kernel(**inputs):
    import numpy as _np
    import concourse.bacc as _bacc
    from concourse import mybir as _mybir
    from concourse.bass_utils import run_bass_kernel_spmd as _run

    nc = _bacc.Bacc("TRN2", target_bir_lowering=False, num_devices=1)
    arrays, args = {}, []
    for name in _INS:
        a = _np.ascontiguousarray(inputs[name])
        arrays[f"in_{name}_dram"] = a
        args.append(nc.dram_tensor(f"in_{name}_dram", a.shape, _mybir.dt.from_np(a.dtype), kind="ExternalInput").ap())
    consts = _constants(_np)
    arrays["consts_dram"] = consts
    args.append(nc.dram_tensor("consts_dram", consts.shape, _mybir.dt.float32, kind="ExternalInput").ap())
    args.append(nc.dram_tensor("out_0_dram", (2048, 1), _mybir.dt.float32, kind="ExternalOutput").ap())
    attention_recommender_kernel(nc, *args)
    r = _run(nc, [arrays], core_ids=[0])
    return r.results[0]["out_0_dram"]
```

```python
import concourse.bass as bass
from concourse import mybir
from contextlib import ExitStack


def attention_recommender_kernel(
    nc: bass.Bass,
    x: bass.AP,
    emb_table: bass.AP,
    Wq: bass.AP,
    Wk: bass.AP,
    Wv: bass.AP,
    final_w: bass.AP,
    W1: bass.AP,
    b1: bass.AP,
    W2: bass.AP,
    b2: bass.AP,
    W3: bass.AP,
    b3: bass.AP,
    consts: bass.AP,
    out: bass.AP,
):
    fp32 = mybir.dt.float32
    i32 = mybir.dt.int32
    f32r = mybir.dt.float32r
    ALU = mybir.AluOpType
    ACT = mybir.ActivationFunctionType
    AX = mybir.AxisListType

    B, F = x.shape
    E = emb_table.shape[1]
    L = Wq.shape[0]
    HID = W1.shape[1]
    H = 2
    DH = E // H
    P = 128
    Q = 32
    QB = P // Q
    SB = 16
    T = SB // QB
    NS = 4
    ITB = NS * SB
    NI = B // ITB
    JOBS = L * NS
    LAST = NI - 1
    ROWS = SB * F
    GPS = ROWS // P
    NG = B * F // P
    FULL = JOBS - NS
    PREP = FULL
    DNN0 = 4
    DNN_SLOTS = 3
    FM = F // QB
    CH = 512

    x_rows = x.rearrange("b f -> (b f)").rearrange("(c n p) -> n c p", c=NG // P, p=P)
    w1_v = W1.rearrange("(f e) h -> e f h", f=F)
    fw_v = final_w.rearrange("(f e) o -> f (e o)", f=F)

    ctx = ExitStack()
    with ctx:
        def sb(name, shape, dt=fp32):
            return ctx.enter_context(nc.sbuf_tensor(name, shape, dt))

        def pb(name, shape):
            return ctx.enter_context(nc.psum_tensor(name, shape, fp32))

        def sem(name):
            return ctx.enter_context(nc.semaphore(name))

        cst = sb("cst", [P, P + HID + 3 + QB * Q])
        ident = cst[:, 0:P]
        fold = cst[:, P:P + HID]
        field_base = cst[:, P + HID:P + HID + 3]
        quad_sel = cst[:, P + HID + 3:].rearrange("p (q n) -> p q n", q=QB)
        wq_sb = sb("wq_sb", [P, L, E])
        wk_sb = sb("wk_sb", [P, L, E])
        wv_sb = sb("wv_sb", [P, L, E])
        wqT = sb("wqT", [P, L, E])
        wkT = sb("wkT", [P, L, E])
        mT_high = sb("mT_high", [P, L, H, E], f32r)
        mT_low = sb("mT_low", [P, L, H, E], f32r)
        w1_sb = sb("w1_sb", [P, F, HID])
        fw_rows = sb("fw_rows", [F, E])
        fwT = sb("fwT", [P, F])
        wvT = sb("wvT", [P, E])
        mark_w = sb("mark_w", [P, H, Q])
        b1_sb = sb("b1_sb", [P, 1])
        b2_sb = sb("b2_sb", [P, 1])
        b3_sb = sb("b3_sb", [P, 1])
        w2_blocks = sb("w2_blocks", [P, P])
        w3_col = sb("w3_col", [P, 1])
        w3_blocks = sb("w3_blocks", [P, P])
        ones = sb("ones", [P, Q])
        x_int = sb("x_int", [P, NG // P, P], i32)
        x_f = sb("x_f", [P, NG // P, P])
        ids = sb("ids", [P, NG], i32)
        ids_now = sb("ids_now", [P, NS * GPS], i32)
        rows = sb("rows", [P, NS * GPS, E])
        eT = sb("eT", [P, NS, SB, Q])
        attT = sb("attT", [P, NS, SB, Q])
        high = sb("high", [P, 2, ROWS], f32r)
        low = sb("low", [P, 2, ROWS], f32r)
        keys = sb("keys", [P, H, SB, F])
        values = sb("values", [P, 3, T, E])
        centred = sb("centred", [P, 2, T * H, F])
        probs = sb("probs", [P, 2, T * H, Q])
        probsT = sb("probsT", [P, 2, T * H, Q])
        blocks = sb("blocks", [P, 3, T * H, QB, F])
        marks = sb("marks", [P, 2, T * H, F])
        marked = sb("marked", [P, T * H, F])
        mark_sum = sb("mark_sum", [P, T * H])
        row_max = sb("row_max", [P, T * H])
        row_sum = sb("row_sum", [P, 2, T * H])
        row_inv = sb("row_inv", [P, 2, T * H])
        weighted = sb("weighted", [P, 2, SB, F])
        att_part = sb("att_part", [P, B])
        mark_part = sb("mark_part", [P, B // QB, H])
        quad_part = sb("quad_part", [P, B // QB])
        h1_part = sb("h1_part", [P, B])
        h1 = sb("h1", [P, CH])
        h2 = sb("h2", [P, CH])
        dnn = sb("dnn", [P, CH])
        logit = sb("logit", [P, CH])
        y = sb("y", [P, CH])

        keys_ps = pb("keys_ps", [P, H, 512])
        values_ps = pb("values_ps", [P, T, E])
        scores_ps = pb("scores_ps", [P, 2, 512])
        out_ps = pb("out_ps", [P, 512])
        turn_ps = pb("turn_ps", [P, 512])
        dnn_ps = pb("dnn_ps", [P, 512])

        loaded = sem("loaded")
        tail_loaded = sem("tail_loaded")
        x_loaded = sem("x_loaded")
        cst_loaded = sem("cst_loaded")
        zeroed = sem("zeroed")
        x_float = sem("x_float")
        x_turned = sem("x_turned")
        ids_ready = sem("ids_ready")
        w_turned = sem("w_turned")
        w_copied = sem("w_copied")
        m_done = sem("m_done")
        m_high = sem("m_high")
        fw_copied = sem("fw_copied")
        m_copied = sem("m_copied")
        ids_copied = sem("ids_copied")
        high_done = sem("high_done")
        low_done = sem("low_done")
        w3_done = sem("w3_done")
        gathered = [sem(f"gathered{s}") for s in range(NS)]
        rows_turned = sem("rows_turned")
        rows_free = sem("rows_free")
        e_copied = sem("e_copied")
        keys_done = sem("keys_done")
        keys_copied = sem("keys_copied")
        values_done = sem("values_done")
        values_copied = sem("values_copied")
        scores_done = sem("scores_done")
        maxed = sem("maxed")
        centred_done = sem("centred_done")
        exp_done = sem("exp_done")
        summed = sem("summed")
        inverted = sem("inverted")
        normed = sem("normed")
        probs_turned = sem("probs_turned")
        blocks_done = sem("blocks_done")
        out_done = sem("out_done")
        att_done = sem("att_done")
        weighted_done = sem("weighted_done")
        marked_done = sem("marked_done")
        mark_summed = sem("mark_summed")
        mark_part_done = sem("mark_part_done")
        quad_part_done = sem("quad_part_done")
        part_done = sem("part_done")
        dnn_done = sem("dnn_done")
        dnn_copied = sem("dnn_copied")
        tail_pe = sem("tail_pe")
        h1_done = sem("h1_done")
        h2_done = sem("h2_done")
        sig_done = sem("sig_done")
        logit_done = sem("logit_done")
        y_done = sem("y_done")
        stored = sem("stored")

        N_ZEROED = 8

        def jobs(i, c):
            return i * JOBS + c + 1

        def full_jobs(i, c):
            return (i + c // JOBS) * FULL + min(c % JOBS + 1, FULL)

        def last_jobs(i, c):
            return (i + c // JOBS) * NS + max(c % JOBS + 1 - FULL, 0)

        def is_full(c):
            return c % JOBS < FULL

        block = ctx.enter_context(nc.Block())

        @block.sync
        def _(sp):
            sp.dma_start(x_int[:], x_rows).then_inc(x_loaded, 16)
            sp.dma_start(cst[:], consts).then_inc(cst_loaded, 16)
            sp.dma_start(wq_sb[:], Wq.rearrange("l e n -> e l n")).then_inc(loaded, 16)
            sp.dma_start(wk_sb[:], Wk.rearrange("l e n -> e l n")).then_inc(loaded, 16)
            sp.dma_start(fw_rows[:], fw_v).then_inc(loaded, 16)
            sp.dma_start(wv_sb[:], Wv.rearrange("l e n -> e l n")).then_inc(loaded, 16)
            sp.dma_start(w1_sb[:], w1_v).then_inc(loaded, 16)
            sp.dma_start(b3_sb[:], b3[None, :].to_broadcast([P, 1])).then_inc(loaded, 16)
            sp.wait_ge(zeroed, N_ZEROED)
            for c in range(P // HID):
                p = slice(c * HID, (c + 1) * HID)
                sp.dma_start(w2_blocks[p, p], W2).then_inc(tail_loaded, 16)
                sp.dma_start(w3_col[p, :], W3).then_inc(tail_loaded, 16)
                sp.dma_start(b1_sb[p, :], b1[:, None]).then_inc(tail_loaded, 16)
                sp.dma_start(b2_sb[p, :], b2[:, None]).then_inc(tail_loaded, 16)
            sp.wait_ge(y_done, 1)
            sp.dma_start(out.rearrange("(c n) o -> c (n o)", n=CH), y[0:P:Q, :]).then_inc(stored, 16)
            sp.wait_ge(stored, 16)

        N_LOADED = 16 * 6
        N_TAIL_LOADED = 16 * 4 * (P // HID)

        @block.gpsimd
        def _(pool):
            def gather_iteration(i, first):
                if not first:
                    pool.wait_ge(gathered[NS - 1], 16 * GPS * i)
                nc.gpsimd.tensor_copy(ids_now[:], ids[:, bass.ds(i * (NS * GPS), NS * GPS)]).then_inc(ids_copied, 1)
                pool.wait_ge(ids_copied, i + 1)
                for s in range(NS):
                    if not first:
                        pool.wait_ge(rows_turned, (i - 1) * NS + s + 1)
                        pool.sem_inc(rows_free, 1)
                    for k in range(GPS):
                        nc.gpsimd.indirect_dma_start(
                            out=rows[:, s * GPS + k, :], out_offset=None, in_=emb_table,
                            in_offset=bass.IndirectOffsetOnAxis(ap=ids_now[:, s * GPS + k:s * GPS + k + 1], axis=0),
                        ).then_inc(gathered[s], 16)

            nc.gpsimd.memset(blocks[:], 0.0).then_inc(zeroed, 1)
            nc.gpsimd.memset(ones[:], 1.0).then_inc(zeroed, 1)
            nc.gpsimd.memset(w2_blocks[:], 0.0).then_inc(zeroed, 1)
            nc.gpsimd.memset(w3_blocks[:], 0.0).then_inc(zeroed, 1)
            pool.wait_ge(ids_ready, 1)
            gather_iteration(0, True)
            pool.wait_ge(ids_ready, NG // P)
            with pool.Fori(1, NI) as i:
                gather_iteration(i, False)

        @block.tensor
        def _(pe):
            def turn_rows(i, s):
                n = i * NS + s
                pe.wait_ge(gathered[s], (i + 1) * (16 * GPS))
                pe.wait_ge(e_copied, n + 1)
                for k in range(GPS):
                    last = nc.tensor.transpose(turn_ps[:, k * P:(k + 1) * P], rows[:, s * GPS + k, :], ident)
                last.then_inc(rows_turned, 1)

            def slot(i, c, first=False, drain=False):
                if not (first and c < 3) and not drain and is_full(c - 3):
                    b = (c - 3) % JOBS
                    pe.wait_ge(blocks_done, full_jobs(i, c - 3))
                    pe.wait_ge(values_copied, jobs(i, c - 3))
                    if not (first and c < 4):
                        pe.wait_ge(att_done, full_jobs(i, c - 4))
                    for t in range(T):
                        for h in range(H):
                            last = nc.tensor.matmul(
                                out_ps[h * DH:(h + 1) * DH, t * QB * F:(t + 1) * QB * F],
                                values[:, b % 3, t, h * DH:(h + 1) * DH],
                                blocks[:, b % 3, t * H + h, :, :], start=True, stop=True)
                    last.then_inc(out_done, 1)
                if not (first and c < 1):
                    b = (c - 1) % JOBS
                    src = eT if b < NS else attT
                    st = b % NS
                    pe.wait_ge(keys_copied, jobs(i, c - 1))
                    if not (first and c < 3):
                        pe.wait_ge(centred_done, jobs(i, c - 3))
                    for m in range(SB):
                        q, t = m % QB, m // QB
                        last = nc.tensor.matmul(
                            scores_ps[q * Q:(q + 1) * Q, b % 2, t * H * F:(t + 1) * H * F].rearrange(
                                "p (h g) -> p h g", h=H),
                            src[:, st, m, :], keys[:, :, m, :], start=True, stop=True)
                    last.then_inc(scores_done, 1)
                if drain:
                    return
                lay, st = c // NS, c % NS
                src = eT if lay == 0 else attT
                pe.wait_ge(low_done, jobs(i, c))
                for h in range(H):
                    passes = ((mT_high, high), (mT_high, low), (mT_low, high))
                    for n, (m_part, in_part) in enumerate(passes):
                        last = nc.tensor.matmul(keys_ps[:, h, 0:ROWS], m_part[:, lay, h, :], in_part[:, c % 2, :],
                                                start=(n == 0), stop=(n == len(passes) - 1))
                    last.then_inc(keys_done, 1)
                if not (first and c < 1):
                    pe.wait_ge(values_copied, jobs(i, c - 1))
                if lay == 0:
                    pe.wait_ge(e_copied, i * NS + st + 2)
                else:
                    pe.wait_ge(att_done, full_jobs(i, c - NS))
                if is_full(c):
                    for t in range(T):
                        last = nc.tensor.matmul(
                            values_ps[:, t, :], src[:, st, t * QB:(t + 1) * QB, :].rearrange("p b f -> p (b f)"),
                            wv_sb[:, lay, :], start=True, stop=True)
                else:
                    for h in range(H):
                        for q in range(QB):
                            last = nc.tensor.matmul(
                                values_ps[q * Q:(q + 1) * Q, :, h * F:(h + 1) * F],
                                mark_w[:, h, :], src[:, st, q:SB:QB, 0:F], start=True, stop=True)
                last.then_inc(values_done, 1)
                if DNN0 <= c < DNN0 + DNN_SLOTS:
                    if c == DNN0 and not first:
                        pe.wait_ge(dnn_copied, i)
                    step = FM // DNN_SLOTS
                    for m in range((c - DNN0) * step, (c - DNN0 + 1) * step):
                        for q in range(QB):
                            f = m * QB + q
                            last = nc.tensor.matmul(
                                dnn_ps[q * Q:(q + 1) * Q, 0:ITB], w1_sb[:, f, :],
                                eT[:, :, :, f], start=(m == 0), stop=(m == FM - 1))
                    if c == DNN0 + DNN_SLOTS - 1:
                        last.then_inc(dnn_done, 1)

            pe.wait_ge(cst_loaded, 16)
            for c in range(NG // P):
                pe.wait_ge(x_float, c + 1)
                if c:
                    pe.wait_ge(ids_ready, c)
                nc.tensor.transpose(turn_ps[:, 0:P], x_f[:, c, :], ident).then_inc(x_turned, 1)
            pe.wait_ge(loaded, N_LOADED)
            for lay in range(L):
                if lay:
                    pe.wait_ge(w_copied, lay)
                nc.tensor.transpose(out_ps[:, 0:P], wq_sb[:, lay, :], ident)
                nc.tensor.transpose(out_ps[:, P:2 * P], wk_sb[:, lay, :], ident).then_inc(w_turned, 1)
                pe.wait_ge(w_copied, lay + 1)
                if lay:
                    pe.wait_ge(m_copied, lay)
                for h in range(H):
                    last = nc.tensor.matmul(keys_ps[:, h, 0:E], wkT[h * DH:(h + 1) * DH, lay, :],
                                            wqT[h * DH:(h + 1) * DH, lay, :], start=True, stop=True)
                last.then_inc(m_done, 1)
            pe.wait_ge(ids_ready, NG // P)
            nc.tensor.transpose(turn_ps[:, 0:F], fw_rows[:, :], ident[0:F, 0:F])
            nc.tensor.transpose(turn_ps[:, P:2 * P], wv_sb[:, L - 1, :], ident).then_inc(m_done, 1)
            pe.wait_ge(m_copied, L)
            pe.wait_ge(fw_copied, 1)
            for h in range(H):
                d = slice(h * DH, (h + 1) * DH)
                last = nc.tensor.matmul(keys_ps[:, h, 0:F], wvT[d, :], fwT[d, :], start=True, stop=True)
            last.then_inc(m_done, 1)
            pe.wait_ge(zeroed, N_ZEROED)
            turn_rows(0, 0)
            for c in range(JOBS):
                slot(0, c, first=True)
                if c < NS - 1:
                    turn_rows(0, c + 1)
                if c >= PREP:
                    turn_rows(1, c - PREP)
            with pe.Fori(1, LAST) as i:
                for c in range(JOBS):
                    slot(i, c)
                    if c >= PREP:
                        turn_rows(i + 1, c - PREP)
            for c in range(JOBS):
                slot(LAST, c)
            slot(LAST, JOBS, drain=True)

            pe.wait_ge(dnn_copied, NI)
            pe.wait_ge(tail_loaded, N_TAIL_LOADED)
            pe.wait_ge(w3_done, 1)
            for c in range(B // CH):
                last = nc.tensor.matmul(keys_ps[c * Q:(c + 1) * Q, 0, :], fold, h1_part[:, c * CH:(c + 1) * CH],
                                        start=True, stop=True)
            last.then_inc(tail_pe, 1)
            pe.wait_ge(part_done, NI * NS)
            pe.wait_ge(quad_part_done, 1)
            for c in range(B // CH):
                nc.tensor.matmul(out_ps[c * Q:(c + 1) * Q, :], ones[:], att_part[:, c * CH:(c + 1) * CH],
                                 start=True, stop=False)
                for q in range(QB):
                    nc.tensor.matmul(out_ps[c * Q:(c + 1) * Q, q:CH:QB], quad_sel[:, q, :],
                                     quad_part[:, c * CH // QB:(c + 1) * CH // QB], start=False, stop=(q == QB - 1))
            pe.wait_ge(h1_done, 1)
            nc.tensor.matmul(keys_ps[:, 1, :], w2_blocks[:], h1[:], start=True, stop=True).then_inc(tail_pe, 1)
            pe.wait_ge(h2_done, 1)
            nc.tensor.matmul(turn_ps[:, :], w3_blocks[:], h2[:], start=True, stop=True).then_inc(tail_pe, 1)

        @block.scalar
        def _(act):
            def copy_rows(i, s, first):
                act.wait_ge(rows_turned, i * NS + s + 1)
                if not first:
                    act.wait_ge(dnn_done, i)
                    act.wait_ge(att_done, full_jobs(i - 1, s))
                nc.scalar.copy(eT[:, s, :, 0:F],
                               turn_ps[:, 0:ROWS].rearrange("p (b f) -> p b f", b=SB)).then_inc(e_copied, 1)

            def high_part(i, c, first=False):
                st = c % NS
                if c % JOBS < NS:
                    src = eT
                    act.wait_ge(e_copied, (i + c // JOBS) * NS + st + 2)
                else:
                    src = attT
                    act.wait_ge(att_done, full_jobs(i, c - NS))
                if not (first and c < 2):
                    act.wait_ge(keys_done, jobs(i, c - 2) * H)
                nc.scalar.copy(high[:, c % 2, :].rearrange("p (b f) -> p b f", b=SB),
                               src[:, st, :, 0:F]).then_inc(high_done, 1)

            def slot(i, c, first=False, drain=False, last_it=False):
                if not (first and c < 1):
                    b = (c - 1) % JOBS
                    act.wait_ge(values_done, jobs(i, c - 1))
                    if is_full(c - 1):
                        if not (first and c < 4):
                            act.wait_ge(out_done, full_jobs(i, c - 4))
                        nc.scalar.copy(values[:, b % 3, :, :], values_ps[:, :, :]).then_inc(values_copied, 1)
                    else:
                        if not (first and c - 3 < FULL):
                            act.wait_ge(marked_done, last_jobs(i, c - 3))
                        nc.scalar.copy(marks[:, b % 2, :, :].rearrange("p (t h) g -> p t (h g)", t=T),
                                       values_ps[:, :, 0:H * F]).then_inc(values_copied, 1)
                late = first and c < NS - 1
                early = (c + 1) % JOBS < NS
                next_high = not (drain or late or (c == JOBS - 1 and last_it))
                if next_high and early:
                    high_part(i, c + 1, first)
                if not (first and c < 2) and is_full(c - 2):
                    b = (c - 2) % JOBS
                    act.wait_ge(probs_turned, full_jobs(i, c - 2))
                    if not (first and c < 5):
                        act.wait_ge(out_done, full_jobs(i, c - 5))
                    for q in range(QB):
                        p = slice(q * Q, (q + 1) * Q)
                        last = nc.scalar.copy(blocks[p, b % 3, :, q, :], probsT[p, b % 2, :, 0:F])
                    last.then_inc(blocks_done, 1)
                def exponentials():
                    b = (c - 1) % JOBS
                    act.wait_ge(centred_done, jobs(i, c - 1))
                    if not (first and c < 3):
                        if is_full(c - 3):
                            act.wait_ge(probs_turned, full_jobs(i, c - 3))
                        else:
                            act.wait_ge(mark_summed, last_jobs(i, c - 3))
                    nc.scalar.activation(probs[:, b % 2, :, 0:F], centred[:, b % 2, :, :],
                                         ACT.Exp).then_inc(exp_done, 1)

                behind_output = is_full(c - 2)
                if not (first and c < 1) and (behind_output or drain):
                    exponentials()
                if drain:
                    return
                if next_high and not early:
                    high_part(i, c + 1, first)
                if not (first and c < 1):
                    act.wait_ge(scores_done, jobs(i, c - 1))
                act.wait_ge(keys_done, (jobs(i, c) - 1) * H + 1)
                nc.scalar.copy(keys[:, 0, :, :].rearrange("p b f -> p (b f)"), keys_ps[:, 0, 0:ROWS])
                if not (first and c < 1) and not behind_output:
                    exponentials()
                act.wait_ge(keys_done, jobs(i, c) * H)
                nc.scalar.copy(keys[:, 1, :, :].rearrange("p b f -> p (b f)"), keys_ps[:, 1, 0:ROWS]).then_inc(keys_copied, 1)
                if c == DNN0 + DNN_SLOTS:
                    act.wait_ge(dnn_done, i + 1)
                    nc.scalar.copy(h1_part[:, bass.ds(i * ITB, ITB)], dnn_ps[:, 0:ITB]).then_inc(dnn_copied, 1)

            for lay in range(L):
                act.wait_ge(w_turned, lay + 1)
                nc.scalar.copy(wqT[:, lay, :], out_ps[:, 0:P])
                nc.scalar.copy(wkT[:, lay, :], out_ps[:, P:2 * P]).then_inc(w_copied, 1)
                act.wait_ge(m_done, lay + 1)
                nc.scalar.copy(mT_high[:, lay, :, :], keys_ps[:, :, 0:E]).then_inc(m_high, 1)
            act.wait_ge(m_done, L + 1)
            nc.scalar.copy(fwT[:], turn_ps[:, 0:F]).then_inc(e_copied, 1)
            nc.scalar.copy(wvT[:], turn_ps[:, P:2 * P]).then_inc(fw_copied, 1)
            act.wait_ge(m_done, L + 2)
            nc.scalar.copy(mark_w[:, :, 0:F], keys_ps[:, :, 0:F]).then_inc(m_high, 1)
            act.wait_ge(zeroed, N_ZEROED)
            copy_rows(0, 0, True)
            high_part(0, 0, first=True)
            for c in range(JOBS):
                slot(0, c, first=True)
                if c < NS - 1:
                    copy_rows(0, c + 1, True)
                    high_part(0, c + 1, first=True)
                if c >= PREP:
                    copy_rows(1, c - PREP, False)
            with act.Fori(1, LAST) as i:
                for c in range(JOBS):
                    slot(i, c)
                    if c >= PREP:
                        copy_rows(i + 1, c - PREP, False)
            for c in range(JOBS):
                slot(LAST, c, last_it=True)
            slot(LAST, JOBS, drain=True)

            act.wait_ge(tail_pe, 1)
            nc.scalar.activation(h1[:], keys_ps[:, 0, :], ACT.Relu, bias=b1_sb[:]).then_inc(h1_done, 1)
            act.wait_ge(tail_pe, 2)
            nc.scalar.activation(h2[:], keys_ps[:, 1, :], ACT.Relu, bias=b2_sb[:]).then_inc(h2_done, 1)
            act.wait_ge(tail_pe, 3)
            nc.scalar.activation(dnn[:], turn_ps[:, :], ACT.Sigmoid, bias=b3_sb[:]).then_inc(sig_done, 1)
            act.wait_ge(logit_done, 1)
            nc.scalar.activation(y[:], logit[:], ACT.Sigmoid).then_inc(y_done, 1)

        @block.vector
        def _(dve):
            def weigh_product(i, s):
                dve.wait_ge(att_done, full_jobs(i, FULL - NS + s))
                nc.vector.tensor_tensor(weighted[:, s % 2, :, :], attT[:, s, :, 0:F],
                                        fwT[:].unsqueeze(1).to_broadcast([P, SB, F]),
                                        ALU.mult).then_inc(weighted_done, 1)

            def weigh_sum(i, s):
                dve.wait_ge(weighted_done, i * NS + s + 1)
                nc.vector.reduce_sum(att_part[:, bass.ds(i * ITB + s * SB, SB)], weighted[:, s % 2, :, :],
                                     axis=AX.X).then_inc(part_done, 1)

            weighings = {8: [(weigh_product, 0, 0)], 9: [(weigh_sum, 0, 0), (weigh_product, 0, 1)], 3: [(weigh_sum, 1, 1)],
                         4: [(weigh_product, 1, 2)], 5: [(weigh_product, 1, 3), (weigh_sum, 1, 2)],
                         6: [(weigh_sum, 1, 3)]}

            def low_part(i, c):
                src = eT if c % JOBS < NS else attT
                dve.wait_ge(high_done, jobs(i, c))
                nc.vector.tensor_tensor(low[:, c % 2, :].rearrange("p (b f) -> p b f", b=SB), src[:, c % NS, :, 0:F],
                                        high[:, c % 2, :].rearrange("p (b f) -> p b f", b=SB),
                                        ALU.subtract).then_inc(low_done, 1)

            def exponential_sums(i, c, b):
                dve.wait_ge(exp_done, jobs(i, c - 1))
                nc.vector.reduce_sum(row_sum[:, b, :], probs[:, b, :, 0:F], axis=AX.X).then_inc(summed, 1)

            def norm(i, c, b):
                dve.wait_ge(summed, jobs(i, c - 1))
                nc.vector.reciprocal(row_inv[:, b, :], row_sum[:, b, :]).then_inc(inverted, 1)
                dve.wait_ge(inverted, jobs(i, c - 1))
                nc.vector.tensor_tensor(probs[:, b, :, 0:F], probs[:, b, :, 0:F],
                                        row_inv[:, b, :].unsqueeze(2).to_broadcast([P, T * H, F]),
                                        ALU.mult).then_inc(normed, 1)

            def turn_probs(i, c, first):
                dve.wait_ge(normed, full_jobs(i, c))
                if not (first and c < 2):
                    dve.wait_ge(blocks_done, full_jobs(i, c - 2))
                nc.vector.transpose(probsT[:, c % 2, :, :].rearrange("p a g -> p (a g)"),
                                    probs[:, c % 2, :, :].rearrange("p a g -> p (a g)")).then_inc(probs_turned, 1)

            def slot(i, c, first=False, drain=False, last_it=False):
                softmax = not (first and c < 1)
                b = (c - 1) % 2
                sc = scores_ps[:, b, 0:T * H * F].rearrange("p (a g) -> p a g", g=F)
                marking = not (first and c < 2) and not is_full(c - 2)
                b2 = (c - 2) % 2
                early = (c + 1) % JOBS < NS and not (first and c < NS) and not (last_it and c == JOBS - 1)
                if not (first and c < 3) and is_full(c - 2) and c != 2:
                    turn_probs(i, c - 2, first)
                if not drain and (c >= NS or first):
                    low_part(i, c)
                if not (first and c < 3) and is_full(c - 3) and not drain:
                    lay, st = (c - 3) % JOBS // NS, (c - 3) % NS
                    dve.wait_ge(out_done, full_jobs(i, c - 3))
                    nc.vector.tensor_tensor(attT[:, st, :, 0:F],
                                            out_ps[:, 0:ROWS].rearrange("p (b f) -> p b f", b=SB),
                                            (eT if lay == 0 else attT)[:, st, :, 0:F], ALU.add).then_inc(att_done, 1)
                if softmax:
                    dve.wait_ge(scores_done, jobs(i, c - 1))
                    nc.vector.reduce_max(row_max[:], sc, axis=AX.X).then_inc(maxed, 1)
                if marking:
                    dve.wait_ge(exp_done, jobs(i, c - 2))
                    nc.vector.reduce_sum(row_sum[:, b2, :], probs[:, b2, :, 0:F], axis=AX.X).then_inc(summed, 1)
                if softmax:
                    dve.wait_ge(maxed, jobs(i, c - 1))
                    if not (first and c < 3):
                        dve.wait_ge(exp_done, jobs(i, c - 3))
                    nc.vector.tensor_tensor(centred[:, b, :, :], sc,
                                            row_max[:].unsqueeze(2).to_broadcast([P, T * H, F]),
                                            ALU.subtract).then_inc(centred_done, 1)
                if not drain and early:
                    low_part(i, c + 1)
                if marking and softmax and is_full(c - 1):
                    exponential_sums(i, c, b)
                if marking:
                    n = last_jobs(i, c - 2)
                    dve.wait_ge(values_copied, jobs(i, c - 2))
                    nc.vector.tensor_tensor(marked[:], probs[:, b2, :, 0:F], marks[:, b2, :, :],
                                            ALU.mult).then_inc(marked_done, 1)
                    dve.wait_ge(summed, jobs(i, c - 2))
                    nc.vector.reciprocal(row_inv[:, b2, :], row_sum[:, b2, :]).then_inc(inverted, 1)
                    if softmax and is_full(c - 1):
                        norm(i, c, b)
                    dve.wait_ge(marked_done, n)
                    nc.vector.reduce_sum(mark_sum[:], marked[:], axis=AX.X).then_inc(mark_summed, 1)
                if not drain:
                    for step, back, s in weighings.get(c, []):
                        if not (first and back):
                            step(i - back, s)
                if c == 1 and marking:
                    turn_probs(i, 0, first)
                if marking:
                    dve.wait_ge(mark_summed, n)
                    dve.wait_ge(inverted, jobs(i, c - 2))
                    nc.vector.tensor_tensor(mark_part[:, bass.ds((n - 1) * T, T), :].rearrange("p t h -> p (t h)"),
                                            mark_sum[:], row_inv[:, b2, :], ALU.mult).then_inc(mark_part_done, 1)
                if softmax and is_full(c - 1) and not marking:
                    exponential_sums(i, c, b)
                    norm(i, c, b)
                    if c == 1:
                        turn_probs(i, 0, first)

            def last_marks():
                n, b = NI * NS, (JOBS - 1) % 2
                dve.wait_ge(exp_done, NI * JOBS)
                nc.vector.reduce_sum(row_sum[:, b, :], probs[:, b, :, 0:F], axis=AX.X).then_inc(summed, 1)
                dve.wait_ge(values_copied, NI * JOBS)
                nc.vector.tensor_tensor(marked[:], probs[:, b, :, 0:F], marks[:, b, :, :], ALU.mult).then_inc(marked_done, 1)
                dve.wait_ge(summed, NI * JOBS)
                nc.vector.reciprocal(row_inv[:, b, :], row_sum[:, b, :]).then_inc(inverted, 1)
                dve.wait_ge(marked_done, n)
                nc.vector.reduce_sum(mark_sum[:], marked[:], axis=AX.X).then_inc(mark_summed, 1)
                dve.wait_ge(mark_summed, n)
                dve.wait_ge(inverted, NI * JOBS)
                nc.vector.tensor_tensor(mark_part[:, (n - 1) * T:n * T, :].rearrange("p t h -> p (t h)"),
                                        mark_sum[:], row_inv[:, b, :], ALU.mult).then_inc(mark_part_done, 1)

            dve.wait_ge(x_loaded, 16)
            for c in range(NG // P):
                nc.vector.tensor_copy(x_f[:, c, :], x_int[:, c, :]).then_inc(x_float, 1)
            dve.wait_ge(cst_loaded, 16)
            for c in range(NG // P):
                dve.wait_ge(x_turned, c + 1)
                for r in range(3):
                    first_col = (r - c * P) % 3
                    last = nc.vector.tensor_scalar(ids[:, c * P + first_col:(c + 1) * P:3],
                                                   turn_ps[:, first_col:P:3],
                                                   field_base[:, r:r + 1], None, ALU.add)
                last.then_inc(ids_ready, 1)
            nc.vector.memset(eT[:, :, :, F:Q], 0.0).then_inc(zeroed, 1)
            nc.vector.memset(attT[:, :, :, F:Q], 0.0).then_inc(zeroed, 1)
            nc.vector.memset(probs[:, :, :, F:Q], 0.0).then_inc(zeroed, 1)
            nc.vector.memset(mark_w[:, :, F:Q], 0.0).then_inc(zeroed, 1)
            dve.wait_ge(zeroed, N_ZEROED)
            for lay in range(L):
                dve.wait_ge(m_high, lay + 1)
                nc.vector.tensor_tensor(mT_low[:, lay, :, :], keys_ps[:, :, 0:E], mT_high[:, lay, :, :],
                                        ALU.subtract).then_inc(m_copied, 1)
            dve.wait_ge(m_high, L + 1)
            for c in range(JOBS):
                slot(0, c, first=True)
            with dve.Fori(1, LAST) as i:
                for c in range(JOBS):
                    slot(i, c)
            for c in range(JOBS + 1):
                slot(LAST, c, drain=(c >= JOBS), last_it=True)
            weigh_sum(LAST, 1)
            for s in range(2, NS):
                dve.wait_ge(part_done, LAST * NS + s)
                weigh_product(LAST, s)
                weigh_sum(LAST, s)
            last_marks()
            dve.wait_ge(mark_part_done, NI * NS)
            nc.vector.tensor_tensor(quad_part[:], mark_part[:, :, 0], mark_part[:, :, 1], ALU.add).then_inc(quad_part_done, 1)
            dve.wait_ge(tail_loaded, N_TAIL_LOADED)
            for c in range(P // HID):
                p = slice(c * HID, (c + 1) * HID)
                last = nc.vector.tensor_copy(w3_blocks[p, p], w3_col[p, :].to_broadcast([HID, HID]))
            last.then_inc(w3_done, 1)
            dve.wait_ge(sig_done, 1)
            nc.vector.tensor_tensor(logit[:], out_ps[:, :], dnn[:], ALU.add).then_inc(logit_done, 1)


_INS = ['r_x', 'L0_rec_emb_table', 'L0_rec_Wq', 'L0_rec_Wk', 'L0_rec_Wv', 'L0_rec_final_w', 'L0_rec_W1',
        'L0_rec_b1', 'L0_rec_W2', 'L0_rec_b2', 'L0_rec_W3', 'L0_rec_b3']


def _constants(np):
    P, HID, F, DIM = 128, 32, 24, 1000
    ident = np.eye(P, dtype=np.float32)
    fold = np.tile(np.eye(HID, dtype=np.float32), (P // HID, 1))
    p = np.arange(P)
    base = np.stack([((P * n + p) % F) * DIM for n in range(3)], axis=1).astype(np.float32)
    quads = np.repeat(np.repeat(np.eye(P // HID, dtype=np.float32), HID, axis=0), HID, axis=1)
    return np.ascontiguousarray(np.concatenate([ident, fold, base, quads], axis=1))


def kernel(**inputs):
    import numpy as _np
    import concourse.bacc as _bacc
    from concourse import mybir as _mybir
    from concourse.bass_utils import run_bass_kernel_spmd as _run

    nc = _bacc.Bacc("TRN2", target_bir_lowering=False, num_devices=1)
    arrays, args = {}, []
    for name in _INS:
        a = _np.ascontiguousarray(inputs[name])
        arrays[f"in_{name}_dram"] = a
        args.append(nc.dram_tensor(f"in_{name}_dram", a.shape, _mybir.dt.from_np(a.dtype), kind="ExternalInput").ap())
    consts = _constants(_np)
    arrays["consts_dram"] = consts
    args.append(nc.dram_tensor("consts_dram", consts.shape, _mybir.dt.float32, kind="ExternalInput").ap())
    args.append(nc.dram_tensor("out_0_dram", (2048, 1), _mybir.dt.float32, kind="ExternalOutput").ap())
    attention_recommender_kernel(nc, *args)
    r = _run(nc, [arrays], core_ids=[0])
    return r.results[0]["out_0_dram"]
```

```python
import concourse.bass as bass
from concourse import mybir
from contextlib import ExitStack


def attention_recommender_kernel(
    nc: bass.Bass,
    x: bass.AP,
    emb_table: bass.AP,
    Wq: bass.AP,
    Wk: bass.AP,
    Wv: bass.AP,
    final_w: bass.AP,
    W1: bass.AP,
    b1: bass.AP,
    W2: bass.AP,
    b2: bass.AP,
    W3: bass.AP,
    b3: bass.AP,
    consts: bass.AP,
    out: bass.AP,
):
    fp32 = mybir.dt.float32
    i32 = mybir.dt.int32
    f32r = mybir.dt.float32r
    ALU = mybir.AluOpType
    ACT = mybir.ActivationFunctionType
    AX = mybir.AxisListType

    B, F = x.shape
    E = emb_table.shape[1]
    L = Wq.shape[0]
    HID = W1.shape[1]
    H = 2
    DH = E // H
    P = 128
    Q = 32
    QB = P // Q
    SB = 16
    T = SB // QB
    NS = 4
    ITB = NS * SB
    NI = B // ITB
    JOBS = L * NS
    LAST = NI - 1
    ROWS = SB * F
    GPS = ROWS // P
    NG = B * F // P
    FULL = JOBS - NS
    PREP = FULL
    DNN0 = 1
    DNN0_FIRST = 4
    DNN_SLOTS = 3
    DNN_COPY = 7
    FM = F // QB
    CH = 512
    DONE_QUADS = LAST * ITB // QB
    FOLD = 9

    x_rows = x.rearrange("b f -> (b f)").rearrange("(c n p) -> n c p", c=NG // P, p=P)
    w1_v = W1.rearrange("(f e) h -> e f h", f=F)
    fw_v = final_w.rearrange("(f e) o -> f (e o)", f=F)

    ctx = ExitStack()
    with ctx:
        def sb(name, shape, dt=fp32):
            return ctx.enter_context(nc.sbuf_tensor(name, shape, dt))

        def pb(name, shape):
            return ctx.enter_context(nc.psum_tensor(name, shape, fp32))

        def sem(name):
            return ctx.enter_context(nc.semaphore(name))

        cst = sb("cst", [P, P + HID + 3 + QB * Q])
        ident = cst[:, 0:P]
        fold = cst[:, P:P + HID]
        field_base = cst[:, P + HID:P + HID + 3]
        quad_sel = cst[:, P + HID + 3:].rearrange("p (q n) -> p q n", q=QB)
        wq_sb = sb("wq_sb", [P, L, E])
        wk_sb = sb("wk_sb", [P, L, E])
        wv_sb = sb("wv_sb", [P, L, E])
        wqT = sb("wqT", [P, L, E])
        wkT = sb("wkT", [P, L, E])
        mT_high = sb("mT_high", [P, L, H, E], f32r)
        mT_low = sb("mT_low", [P, L, H, E], f32r)
        w1_sb = sb("w1_sb", [P, F, HID])
        fw_rows = sb("fw_rows", [F, E])
        fwT = sb("fwT", [P, F])
        wvT = sb("wvT", [P, E])
        mark_w = sb("mark_w", [P, H, Q])
        b1_sb = sb("b1_sb", [P, 1])
        b2_sb = sb("b2_sb", [P, 1])
        b3_sb = sb("b3_sb", [P, 1])
        w2_blocks = sb("w2_blocks", [P, P])
        w3_col = sb("w3_col", [P, 1])
        w3_blocks = sb("w3_blocks", [P, P])
        ones = sb("ones", [P, Q])
        x_int = sb("x_int", [P, NG // P, P], i32)
        x_f = sb("x_f", [P, NG // P, P])
        ids = sb("ids", [P, NG], i32)
        ids_now = sb("ids_now", [P, NS * GPS], i32)
        rows = sb("rows", [P, NS * GPS, E])
        eT = sb("eT", [P, NS, SB, Q])
        attT = sb("attT", [P, NS, SB, Q])
        high = sb("high", [P, 2, ROWS], f32r)
        low = sb("low", [P, 2, ROWS], f32r)
        keys = sb("keys", [P, H, SB, F])
        values = sb("values", [P, 3, T, E])
        centred = sb("centred", [P, 2, T * H, F])
        probs = sb("probs", [P, 2, T * H, Q])
        probsT = sb("probsT", [P, 2, T * H, Q])
        blocks = sb("blocks", [P, 3, T * H, QB, F])
        marks = sb("marks", [P, 2, T * H, F])
        marked = sb("marked", [P, T * H, F])
        mark_sum = sb("mark_sum", [P, T * H])
        row_max = sb("row_max", [P, T * H])
        row_sum = sb("row_sum", [P, 2, T * H])
        row_inv = sb("row_inv", [P, 2, T * H])
        weighted = sb("weighted", [P, 2, SB, F])
        quad_part = sb("quad_part", [P, DONE_QUADS])
        att_part = sb("att_part", [P, B])
        mark_part = sb("mark_part", [P, B // QB, H])
        h1_part = sb("h1_part", [P, B])
        h1 = sb("h1", [P, CH])
        h2 = sb("h2", [P, CH])
        dnn = sb("dnn", [P, CH])
        logit = sb("logit", [P, CH])
        y = sb("y", [P, CH])

        keys_ps = pb("keys_ps", [P, H, 512])
        values_ps = pb("values_ps", [P, T, E])
        scores_ps = pb("scores_ps", [P, 2, 512])
        out_ps = pb("out_ps", [P, 512])
        turn_ps = pb("turn_ps", [P, 512])
        dnn_ps = pb("dnn_ps", [P, 512])

        loaded = sem("loaded")
        tail_loaded = sem("tail_loaded")
        x_loaded = sem("x_loaded")
        cst_loaded = sem("cst_loaded")
        zeroed = sem("zeroed")
        x_float = sem("x_float")
        x_turned = sem("x_turned")
        ids_ready = sem("ids_ready")
        w_turned = sem("w_turned")
        fw_turned = sem("fw_turned")
        w_copied = sem("w_copied")
        m_half = sem("m_half")
        m_done = sem("m_done")
        m_high = sem("m_high")
        m_copied = sem("m_copied")
        ids_copied = sem("ids_copied")
        high_done = sem("high_done")
        low_done = sem("low_done")
        w3_done = sem("w3_done")
        gathered = [sem(f"gathered{s}") for s in range(NS)]
        rows_turned = sem("rows_turned")
        rows_free = sem("rows_free")
        e_copied = sem("e_copied")
        keys_done = sem("keys_done")
        keys_copied = sem("keys_copied")
        values_done = sem("values_done")
        values_copied = sem("values_copied")
        scores_done = sem("scores_done")
        maxed = sem("maxed")
        centred_done = sem("centred_done")
        exp_done = sem("exp_done")
        summed = sem("summed")
        inverted = sem("inverted")
        normed = sem("normed")
        probs_turned = sem("probs_turned")
        blocks_done = sem("blocks_done")
        out_done = sem("out_done")
        att_done = sem("att_done")
        weighted_done = sem("weighted_done")
        marked_done = sem("marked_done")
        mark_summed = sem("mark_summed")
        mark_part_done = sem("mark_part_done")
        part_done = sem("part_done")
        quad_part_done = sem("quad_part_done")
        dnn_done = sem("dnn_done")
        dnn_copied = sem("dnn_copied")
        tail_pe = sem("tail_pe")
        att_summed = sem("att_summed")
        h1_done = sem("h1_done")
        h2_done = sem("h2_done")
        sig_done = sem("sig_done")
        logit_done = sem("logit_done")
        y_done = sem("y_done")
        stored = sem("stored")

        N_ZEROED = 8

        w_ps = [out_ps, dnn_ps, scores_ps[:, 0, :]]
        m_ps = [keys_ps[:, :, 0:E], scores_ps[:, 1, 0:H * E].rearrange("p (h e) -> p h e", h=H),
                out_ps[:, 0:H * E].rearrange("p (h e) -> p h e", h=H)]
        mark_ps = dnn_ps[:, 0:H * F].rearrange("p (h f) -> p h f", h=H)

        def jobs(i, c):
            return i * JOBS + c + 1

        def full_jobs(i, c):
            return (i + c // JOBS) * FULL + min(c % JOBS + 1, FULL)

        def last_jobs(i, c):
            return (i + c // JOBS) * NS + max(c % JOBS + 1 - FULL, 0)

        def is_full(c):
            return c % JOBS < FULL

        block = ctx.enter_context(nc.Block())

        @block.sync
        def _(sp):
            sp.dma_start(x_int[:], x_rows).then_inc(x_loaded, 16)
            sp.dma_start(cst[:], consts).then_inc(cst_loaded, 16)
            sp.dma_start(wq_sb[:], Wq.rearrange("l e n -> e l n")).then_inc(loaded, 16)
            sp.dma_start(wk_sb[:], Wk.rearrange("l e n -> e l n")).then_inc(loaded, 16)
            sp.dma_start(fw_rows[:], fw_v).then_inc(loaded, 16)
            sp.dma_start(wv_sb[:], Wv.rearrange("l e n -> e l n")).then_inc(loaded, 16)
            sp.dma_start(w1_sb[:], w1_v).then_inc(loaded, 16)
            sp.dma_start(b3_sb[:], b3[None, :].to_broadcast([P, 1])).then_inc(loaded, 16)
            sp.wait_ge(zeroed, N_ZEROED)
            for c in range(P // HID):
                p = slice(c * HID, (c + 1) * HID)
                sp.dma_start(w2_blocks[p, p], W2).then_inc(tail_loaded, 16)
                sp.dma_start(w3_col[p, :], W3).then_inc(tail_loaded, 16)
                sp.dma_start(b1_sb[p, :], b1[:, None]).then_inc(tail_loaded, 16)
                sp.dma_start(b2_sb[p, :], b2[:, None]).then_inc(tail_loaded, 16)
            sp.wait_ge(y_done, 1)
            sp.dma_start(out.rearrange("(c n) o -> c (n o)", n=CH), y[0:P:Q, :]).then_inc(stored, 16)
            sp.wait_ge(stored, 16)

        N_LOADED = 16 * 6
        N_TAIL_LOADED = 16 * 4 * (P // HID)

        @block.gpsimd
        def _(pool):
            def gather_iteration(i, first):
                if not first:
                    pool.wait_ge(gathered[NS - 1], 16 * GPS * i)
                nc.gpsimd.tensor_copy(ids_now[:], ids[:, bass.ds(i * (NS * GPS), NS * GPS)]).then_inc(ids_copied, 1)
                pool.wait_ge(ids_copied, i + 1)
                for s in range(NS):
                    if not first:
                        pool.wait_ge(rows_turned, (i - 1) * NS + s + 1)
                        pool.sem_inc(rows_free, 1)
                    for k in range(GPS):
                        nc.gpsimd.indirect_dma_start(
                            out=rows[:, s * GPS + k, :], out_offset=None, in_=emb_table,
                            in_offset=bass.IndirectOffsetOnAxis(ap=ids_now[:, s * GPS + k:s * GPS + k + 1], axis=0),
                        ).then_inc(gathered[s], 16)

            nc.gpsimd.memset(blocks[:], 0.0).then_inc(zeroed, 1)
            nc.gpsimd.memset(ones[:], 1.0).then_inc(zeroed, 1)
            nc.gpsimd.memset(w2_blocks[:], 0.0).then_inc(zeroed, 1)
            nc.gpsimd.memset(w3_blocks[:], 0.0).then_inc(zeroed, 1)
            pool.wait_ge(ids_ready, 1)
            gather_iteration(0, True)
            pool.wait_ge(ids_ready, NG // P)
            with pool.Fori(1, NI) as i:
                gather_iteration(i, False)

        @block.tensor
        def _(pe):
            def turn_rows(i, s):
                n = i * NS + s
                pe.wait_ge(gathered[s], (i + 1) * (16 * GPS))
                pe.wait_ge(e_copied, n + 1)
                for k in range(GPS):
                    last = nc.tensor.transpose(turn_ps[:, k * P:(k + 1) * P], rows[:, s * GPS + k, :], ident)
                last.then_inc(rows_turned, 1)

            def slot(i, c, first=False, drain=False):
                if not (first and c < 3) and not drain and is_full(c - 3):
                    b = (c - 3) % JOBS
                    pe.wait_ge(blocks_done, full_jobs(i, c - 3))
                    pe.wait_ge(values_copied, jobs(i, c - 3))
                    if not (first and c < 4):
                        pe.wait_ge(att_done, full_jobs(i, c - 4))
                    for t in range(T):
                        for h in range(H):
                            last = nc.tensor.matmul(
                                out_ps[h * DH:(h + 1) * DH, t * QB * F:(t + 1) * QB * F],
                                values[:, b % 3, t, h * DH:(h + 1) * DH],
                                blocks[:, b % 3, t * H + h, :, :], start=True, stop=True)
                    last.then_inc(out_done, 1)
                if not (first and c < 1):
                    b = (c - 1) % JOBS
                    src = eT if b < NS else attT
                    st = b % NS
                    pe.wait_ge(keys_copied, jobs(i, c - 1))
                    if not (first and c < 3):
                        pe.wait_ge(centred_done, jobs(i, c - 3))
                    for m in range(SB):
                        q, t = m % QB, m // QB
                        last = nc.tensor.matmul(
                            scores_ps[q * Q:(q + 1) * Q, b % 2, t * H * F:(t + 1) * H * F].rearrange(
                                "p (h g) -> p h g", h=H),
                            src[:, st, m, :], keys[:, :, m, :], start=True, stop=True)
                    last.then_inc(scores_done, 1)
                if drain:
                    return
                lay, st = c // NS, c % NS
                src = eT if lay == 0 else attT
                pe.wait_ge(low_done, jobs(i, c))
                for h in range(H):
                    passes = ((mT_high, high), (mT_high, low), (mT_low, high))
                    for n, (m_part, in_part) in enumerate(passes):
                        last = nc.tensor.matmul(keys_ps[:, h, 0:ROWS], m_part[:, lay, h, :], in_part[:, c % 2, :],
                                                start=(n == 0), stop=(n == len(passes) - 1))
                    last.then_inc(keys_done, 1)
                if first and c < NS - 1:
                    turn_rows(0, c + 1)
                if not (first and c < 1):
                    pe.wait_ge(values_copied, jobs(i, c - 1))
                if lay == 0:
                    pe.wait_ge(e_copied, i * NS + st + 2)
                else:
                    pe.wait_ge(att_done, full_jobs(i, c - NS))
                if is_full(c):
                    for t in range(T):
                        last = nc.tensor.matmul(
                            values_ps[:, t, :], src[:, st, t * QB:(t + 1) * QB, :].rearrange("p b f -> p (b f)"),
                            wv_sb[:, lay, :], start=True, stop=True)
                else:
                    for h in range(H):
                        for q in range(QB):
                            last = nc.tensor.matmul(
                                values_ps[q * Q:(q + 1) * Q, :, h * F:(h + 1) * F],
                                mark_w[:, h, :], src[:, st, q:SB:QB, 0:F], start=True, stop=True)
                last.then_inc(values_done, 1)
                dnn0 = DNN0_FIRST if first else DNN0
                if dnn0 <= c < dnn0 + DNN_SLOTS:
                    if c == dnn0:
                        pe.wait_ge(e_copied, (i + 1) * NS + 1)
                    if c == dnn0 and not first:
                        pe.wait_ge(dnn_copied, i)
                    step = FM // DNN_SLOTS
                    for m in range((c - dnn0) * step, (c - dnn0 + 1) * step):
                        for q in range(QB):
                            f = m * QB + q
                            last = nc.tensor.matmul(
                                dnn_ps[q * Q:(q + 1) * Q, 0:ITB], w1_sb[:, f, :],
                                eT[:, :, :, f], start=(m == 0), stop=(m == FM - 1))
                    if c == dnn0 + DNN_SLOTS - 1:
                        last.then_inc(dnn_done, 1)

            pe.wait_ge(cst_loaded, 16)
            for c in range(NG // P):
                pe.wait_ge(x_float, c + 1)
                if c:
                    pe.wait_ge(ids_ready, c)
                nc.tensor.transpose(turn_ps[:, 0:P], x_f[:, c, :], ident).then_inc(x_turned, 1)
            pe.wait_ge(loaded, N_LOADED)
            for lay in range(L):
                nc.tensor.transpose(w_ps[lay][:, 0:P], wq_sb[:, lay, :], ident)
                nc.tensor.transpose(w_ps[lay][:, P:2 * P], wk_sb[:, lay, :], ident).then_inc(w_turned, 1)

            def make_m(lay):
                pe.wait_ge(w_copied, lay + 1)
                for h in range(H):
                    if lay and h:
                        pe.wait_ge(m_half, lay)
                    last = nc.tensor.matmul(m_ps[lay][:, h, :], wkT[h * DH:(h + 1) * DH, lay, :],
                                            wqT[h * DH:(h + 1) * DH, lay, :], start=True, stop=True)
                    if lay and not h:
                        last.then_inc(m_half, 1)
                last.then_inc(m_done, 1)

            make_m(0)
            pe.wait_ge(ids_ready, NG // P)
            nc.tensor.transpose(turn_ps[:, 0:F], fw_rows[:, :], ident[0:F, 0:F])
            nc.tensor.transpose(turn_ps[:, P:2 * P], wv_sb[:, L - 1, :], ident).then_inc(fw_turned, 1)
            make_m(1)
            turn_rows(0, 0)
            make_m(2)
            pe.wait_ge(e_copied, 1)
            for h in range(H):
                d = slice(h * DH, (h + 1) * DH)
                if h:
                    pe.wait_ge(m_half, L)
                last = nc.tensor.matmul(mark_ps[:, h, :], wvT[d, :], fwT[d, :], start=True, stop=True)
                if not h:
                    last.then_inc(m_half, 1)
            last.then_inc(m_done, 1)
            pe.wait_ge(zeroed, N_ZEROED)
            pe.wait_ge(m_copied, 1)
            for c in range(JOBS):
                if c == 1:
                    pe.wait_ge(m_copied, L)
                    pe.wait_ge(m_high, L + 1)
                slot(0, c, first=True)
                if c >= PREP:
                    turn_rows(1, c - PREP)
            with pe.Fori(1, LAST) as i:
                for c in range(JOBS):
                    slot(i, c)
                    if c >= PREP:
                        turn_rows(i + 1, c - PREP)
            for c in range(JOBS):
                slot(LAST, c)
                if c == FOLD:
                    pe.wait_ge(dnn_copied, NI)
                    pe.wait_ge(e_copied, NI * NS + 1)
                    for n in range(B // CH):
                        last = nc.tensor.matmul(turn_ps[n * Q:(n + 1) * Q, :], fold, h1_part[:, n * CH:(n + 1) * CH],
                                                start=True, stop=True)
                    last.then_inc(tail_pe, 1)
                if c == FOLD + 1:
                    pe.wait_ge(tail_loaded, N_TAIL_LOADED)
                    pe.wait_ge(h1_done, 1)
                    nc.tensor.matmul(dnn_ps[:, :], w2_blocks[:], h1[:], start=True, stop=True).then_inc(tail_pe, 1)
            slot(LAST, JOBS, drain=True)

            pe.wait_ge(w3_done, 1)
            pe.wait_ge(h2_done, 1)
            nc.tensor.matmul(turn_ps[:, :], w3_blocks[:], h2[:], start=True, stop=True).then_inc(tail_pe, 1)
            pe.wait_ge(att_done, full_jobs(LAST, FULL - 1))
            for c in range(B // CH):
                if c == B // CH - 1:
                    pe.wait_ge(part_done, NI * NS)
                nc.tensor.matmul(out_ps[c * Q:(c + 1) * Q, :], ones[:], att_part[:, c * CH:(c + 1) * CH],
                                 start=True, stop=False)
            pe.wait_ge(quad_part_done, 1)
            for q in range(QB):
                for c in range(B // CH):
                    n = min(CH // QB, DONE_QUADS - c * (CH // QB))
                    nc.tensor.matmul(out_ps[c * Q:(c + 1) * Q, q:n * QB:QB], quad_sel[:, q, :],
                                     quad_part[:, c * (CH // QB):c * (CH // QB) + n],
                                     start=False, stop=(q == QB - 1 and c < B // CH - 1))
            pe.wait_ge(mark_part_done, NI * NS)
            for q in range(QB):
                for h in range(H):
                    last = nc.tensor.matmul(out_ps[P - Q:P, CH - ITB + q:CH:QB], quad_sel[:, q, :],
                                            mark_part[:, DONE_QUADS:, h],
                                            start=False, stop=(q == QB - 1 and h == H - 1))
            last.then_inc(att_summed, 1)

        @block.scalar
        def _(act):
            def copy_rows(i, s, first):
                act.wait_ge(rows_turned, i * NS + s + 1)
                if not first:
                    act.wait_ge(dnn_done, i)
                    act.wait_ge(att_done, full_jobs(i - 1, s))
                nc.scalar.copy(eT[:, s, :, 0:F],
                               turn_ps[:, 0:ROWS].rearrange("p (b f) -> p b f", b=SB)).then_inc(e_copied, 1)

            def high_part(i, c, first=False):
                st = c % NS
                if c % JOBS < NS:
                    src = eT
                    act.wait_ge(e_copied, (i + c // JOBS) * NS + st + 2)
                else:
                    src = attT
                    act.wait_ge(att_done, full_jobs(i, c - NS))
                if not (first and c < 2):
                    act.wait_ge(keys_done, jobs(i, c - 2) * H)
                nc.scalar.copy(high[:, c % 2, :].rearrange("p (b f) -> p b f", b=SB),
                               src[:, st, :, 0:F]).then_inc(high_done, 1)

            def slot(i, c, first=False, drain=False, last_it=False):
                if not (first and c < 1):
                    b = (c - 1) % JOBS
                    act.wait_ge(values_done, jobs(i, c - 1))
                    if is_full(c - 1):
                        if not (first and c < 4):
                            act.wait_ge(out_done, full_jobs(i, c - 4))
                        nc.scalar.copy(values[:, b % 3, :, :], values_ps[:, :, :]).then_inc(values_copied, 1)
                    else:
                        if not (first and c - 3 < FULL):
                            act.wait_ge(marked_done, last_jobs(i, c - 3))
                        nc.scalar.copy(marks[:, b % 2, :, :].rearrange("p (t h) g -> p t (h g)", t=T),
                                       values_ps[:, :, 0:H * F]).then_inc(values_copied, 1)
                late = first and c < NS - 1
                early = (c + 1) % JOBS < NS
                next_high = not (drain or late or (c == JOBS - 1 and last_it))
                if next_high and early:
                    high_part(i, c + 1, first)
                if not (first and c < 2) and is_full(c - 2):
                    b = (c - 2) % JOBS
                    act.wait_ge(probs_turned, full_jobs(i, c - 2))
                    if not (first and c < 5):
                        act.wait_ge(out_done, full_jobs(i, c - 5))
                    for q in range(QB):
                        p = slice(q * Q, (q + 1) * Q)
                        last = nc.scalar.copy(blocks[p, b % 3, :, q, :], probsT[p, b % 2, :, 0:F])
                    last.then_inc(blocks_done, 1)
                def exponentials():
                    b = (c - 1) % JOBS
                    act.wait_ge(centred_done, jobs(i, c - 1))
                    if not (first and c < 3):
                        if is_full(c - 3):
                            act.wait_ge(probs_turned, full_jobs(i, c - 3))
                        else:
                            act.wait_ge(mark_summed, last_jobs(i, c - 3))
                    nc.scalar.activation(probs[:, b % 2, :, 0:F], centred[:, b % 2, :, :],
                                         ACT.Exp).then_inc(exp_done, 1)

                exp_first = is_full(c - 2)
                if not (first and c < 1) and (exp_first or drain):
                    exponentials()
                if drain:
                    return
                if next_high and not early:
                    high_part(i, c + 1, first)
                if not (first and c < 1):
                    act.wait_ge(scores_done, jobs(i, c - 1))
                act.wait_ge(keys_done, (jobs(i, c) - 1) * H + 1)
                nc.scalar.copy(keys[:, 0, :, :].rearrange("p b f -> p (b f)"), keys_ps[:, 0, 0:ROWS])
                if not (first and c < 1) and not exp_first and is_full(c - 1):
                    exponentials()
                act.wait_ge(keys_done, jobs(i, c) * H)
                nc.scalar.copy(keys[:, 1, :, :].rearrange("p b f -> p (b f)"), keys_ps[:, 1, 0:ROWS]).then_inc(keys_copied, 1)
                if not (first and c < 1) and not exp_first and not is_full(c - 1):
                    exponentials()
                if c == DNN_COPY:
                    act.wait_ge(dnn_done, i + 1)
                    nc.scalar.copy(h1_part[:, bass.ds(i * ITB, ITB)], dnn_ps[:, 0:ITB]).then_inc(dnn_copied, 1)

            for lay in range(L):
                act.wait_ge(w_turned, lay + 1)
                nc.scalar.copy(wqT[:, lay, :], w_ps[lay][:, 0:P])
                nc.scalar.copy(wkT[:, lay, :], w_ps[lay][:, P:2 * P]).then_inc(w_copied, 1)

            def high_m(lay):
                act.wait_ge(m_done, lay + 1)
                nc.scalar.copy(mT_high[:, lay, :, :], m_ps[lay]).then_inc(m_high, 1)

            high_m(0)
            act.wait_ge(fw_turned, 1)
            nc.scalar.copy(fwT[:], turn_ps[:, 0:F])
            nc.scalar.copy(wvT[:], turn_ps[:, P:2 * P]).then_inc(e_copied, 1)
            act.wait_ge(zeroed, N_ZEROED)
            copy_rows(0, 0, True)
            high_part(0, 0, first=True)
            high_m(1)
            high_m(2)
            act.wait_ge(m_done, L + 1)
            nc.scalar.copy(mark_w[:, :, 0:F], mark_ps).then_inc(m_high, 1)
            for c in range(JOBS):
                slot(0, c, first=True)
                if c < NS - 1:
                    copy_rows(0, c + 1, True)
                    high_part(0, c + 1, first=True)
                if c >= PREP:
                    copy_rows(1, c - PREP, False)
            with act.Fori(1, LAST) as i:
                for c in range(JOBS):
                    slot(i, c)
                    if c >= PREP:
                        copy_rows(i + 1, c - PREP, False)
            for c in range(JOBS):
                slot(LAST, c, last_it=True)
                if c == FOLD:
                    act.wait_ge(tail_pe, 1)
                    nc.scalar.activation(h1[:], turn_ps[:, :], ACT.Relu, bias=b1_sb[:]).then_inc(h1_done, 1)
                if c == FOLD + 1:
                    act.wait_ge(tail_pe, 2)
                    nc.scalar.activation(h2[:], dnn_ps[:, :], ACT.Relu, bias=b2_sb[:]).then_inc(h2_done, 1)
            slot(LAST, JOBS, drain=True)
            act.wait_ge(tail_pe, 3)
            nc.scalar.activation(dnn[:], turn_ps[:, :], ACT.Sigmoid, bias=b3_sb[:]).then_inc(sig_done, 1)
            act.wait_ge(logit_done, 1)
            nc.scalar.activation(y[:], logit[:], ACT.Sigmoid).then_inc(y_done, 1)

        @block.vector
        def _(dve):
            def weigh_product(i, s):
                dve.wait_ge(att_done, full_jobs(i, FULL - NS + s))
                nc.vector.tensor_tensor(weighted[:, s % 2, :, :], attT[:, s, :, 0:F],
                                        fwT[:].unsqueeze(1).to_broadcast([P, SB, F]),
                                        ALU.mult).then_inc(weighted_done, 1)

            def weigh_sum(i, s):
                dve.wait_ge(weighted_done, i * NS + s + 1)
                nc.vector.reduce_sum(att_part[:, bass.ds(i * ITB + s * SB, SB)], weighted[:, s % 2, :, :],
                                     axis=AX.X).then_inc(part_done, 1)

            weighings = {8: [(weigh_product, 0, 0)],
                         9: [(weigh_sum, 0, 0), (weigh_product, 0, 1)],
                         2: [(weigh_sum, 1, 1)],
                         3: [(weigh_product, 1, 2)],
                         4: [(weigh_sum, 1, 2)],
                         5: [(weigh_product, 1, 3)],
                         6: [(weigh_sum, 1, 3)]}
            last_weighings = {10: [(weigh_sum, 1), (weigh_product, 2)], 11: [(weigh_sum, 2), (weigh_product, 3)]}

            def low_part(i, c):
                src = eT if c % JOBS < NS else attT
                dve.wait_ge(high_done, jobs(i, c))
                nc.vector.tensor_tensor(low[:, c % 2, :].rearrange("p (b f) -> p b f", b=SB), src[:, c % NS, :, 0:F],
                                        high[:, c % 2, :].rearrange("p (b f) -> p b f", b=SB),
                                        ALU.subtract).then_inc(low_done, 1)

            def exponential_sums(i, c, b):
                dve.wait_ge(exp_done, jobs(i, c - 1))
                nc.vector.reduce_sum(row_sum[:, b, :], probs[:, b, :, 0:F], axis=AX.X).then_inc(summed, 1)

            def norm(i, c, b):
                dve.wait_ge(summed, jobs(i, c - 1))
                nc.vector.reciprocal(row_inv[:, b, :], row_sum[:, b, :]).then_inc(inverted, 1)
                dve.wait_ge(inverted, jobs(i, c - 1))
                nc.vector.tensor_tensor(probs[:, b, :, 0:F], probs[:, b, :, 0:F],
                                        row_inv[:, b, :].unsqueeze(2).to_broadcast([P, T * H, F]),
                                        ALU.mult).then_inc(normed, 1)

            def soon(c):
                return c in (3, 8, 10)

            def turn_probs(i, c, first):
                dve.wait_ge(normed, full_jobs(i, c))
                if not (first and c < 2):
                    dve.wait_ge(blocks_done, full_jobs(i, c - 2))
                nc.vector.transpose(probsT[:, c % 2, :, :].rearrange("p a g -> p (a g)"),
                                    probs[:, c % 2, :, :].rearrange("p a g -> p (a g)")).then_inc(probs_turned, 1)

            def slot(i, c, first=False, drain=False, last_it=False):
                softmax = not (first and c < 1)
                b = (c - 1) % 2
                sc = scores_ps[:, b, 0:T * H * F].rearrange("p (a g) -> p a g", g=F)
                marking = not (first and c < 2) and not is_full(c - 2)
                b2 = (c - 2) % 2
                early = (c + 1) % JOBS < NS and not (first and c < NS) and not (last_it and c == JOBS - 1)
                if not (first and c < 3) and is_full(c - 2) and c != 2:
                    turn_probs(i, c - 2, first)
                if not drain and (c >= NS or first) and not soon(c - 1):
                    low_part(i, c)
                if not (first and c < 3) and is_full(c - 3) and not drain:
                    lay, st = (c - 3) % JOBS // NS, (c - 3) % NS
                    dve.wait_ge(out_done, full_jobs(i, c - 3))
                    nc.vector.tensor_tensor(attT[:, st, :, 0:F],
                                            out_ps[:, 0:ROWS].rearrange("p (b f) -> p b f", b=SB),
                                            (eT if lay == 0 else attT)[:, st, :, 0:F], ALU.add).then_inc(att_done, 1)
                if drain:
                    weigh_sum(i, NS - 1)
                if softmax:
                    dve.wait_ge(scores_done, jobs(i, c - 1))
                    nc.vector.reduce_max(row_max[:], sc, axis=AX.X).then_inc(maxed, 1)
                if marking:
                    dve.wait_ge(exp_done, jobs(i, c - 2))
                    nc.vector.reduce_sum(row_sum[:, b2, :], probs[:, b2, :, 0:F], axis=AX.X).then_inc(summed, 1)
                if softmax:
                    dve.wait_ge(maxed, jobs(i, c - 1))
                    if not (first and c < 3):
                        dve.wait_ge(exp_done, jobs(i, c - 3))
                    nc.vector.tensor_tensor(centred[:, b, :, :], sc,
                                            row_max[:].unsqueeze(2).to_broadcast([P, T * H, F]),
                                            ALU.subtract).then_inc(centred_done, 1)
                if not drain and early or soon(c) and not is_full(c - 1):
                    low_part(i, c + 1)
                if marking and softmax and is_full(c - 1):
                    exponential_sums(i, c, b)
                if marking:
                    n = last_jobs(i, c - 2)
                    dve.wait_ge(values_copied, jobs(i, c - 2))
                    nc.vector.tensor_tensor(marked[:], probs[:, b2, :, 0:F], marks[:, b2, :, :],
                                            ALU.mult).then_inc(marked_done, 1)
                    dve.wait_ge(summed, jobs(i, c - 2))
                    nc.vector.reciprocal(row_inv[:, b2, :], row_sum[:, b2, :]).then_inc(inverted, 1)
                    if softmax and is_full(c - 1):
                        norm(i, c, b)
                    dve.wait_ge(marked_done, n)
                    nc.vector.reduce_sum(mark_sum[:], marked[:], axis=AX.X).then_inc(mark_summed, 1)
                if last_it and c == FOLD:
                    dve.wait_ge(mark_part_done, LAST * NS)
                    nc.vector.tensor_tensor(quad_part[:], mark_part[:, 0:DONE_QUADS, 0], mark_part[:, 0:DONE_QUADS, 1],
                                            ALU.add).then_inc(quad_part_done, 1)
                if last_it:
                    for step, s in last_weighings.get(c, []):
                        step(i, s)
                if not drain:
                    for step, back, s in weighings.get(c, []):
                        if not (first and back):
                            step(i - back, s)
                if c == 1 and marking:
                    turn_probs(i, 0, first)
                if marking:
                    dve.wait_ge(mark_summed, n)
                    dve.wait_ge(inverted, jobs(i, c - 2))
                    nc.vector.tensor_tensor(mark_part[:, bass.ds((n - 1) * T, T), :].rearrange("p t h -> p (t h)"),
                                            mark_sum[:], row_inv[:, b2, :], ALU.mult).then_inc(mark_part_done, 1)
                if softmax and is_full(c - 1) and not marking:
                    exponential_sums(i, c, b)
                    if soon(c):
                        low_part(i, c + 1)
                    norm(i, c, b)
                    if c == 1:
                        turn_probs(i, 0, first)

            def last_marks():
                n, b = NI * NS, (JOBS - 1) % 2
                dve.wait_ge(exp_done, NI * JOBS)
                nc.vector.reduce_sum(row_sum[:, b, :], probs[:, b, :, 0:F], axis=AX.X).then_inc(summed, 1)
                dve.wait_ge(values_copied, NI * JOBS)
                nc.vector.tensor_tensor(marked[:], probs[:, b, :, 0:F], marks[:, b, :, :], ALU.mult).then_inc(marked_done, 1)
                dve.wait_ge(summed, NI * JOBS)
                nc.vector.reciprocal(row_inv[:, b, :], row_sum[:, b, :]).then_inc(inverted, 1)
                dve.wait_ge(marked_done, n)
                nc.vector.reduce_sum(mark_sum[:], marked[:], axis=AX.X).then_inc(mark_summed, 1)
                dve.wait_ge(mark_summed, n)
                dve.wait_ge(inverted, NI * JOBS)
                nc.vector.tensor_tensor(mark_part[:, (n - 1) * T:n * T, :].rearrange("p t h -> p (t h)"),
                                        mark_sum[:], row_inv[:, b, :], ALU.mult).then_inc(mark_part_done, 1)

            dve.wait_ge(x_loaded, 16)
            for c in range(NG // P):
                nc.vector.tensor_copy(x_f[:, c, :], x_int[:, c, :]).then_inc(x_float, 1)
            dve.wait_ge(cst_loaded, 16)
            for c in range(NG // P):
                dve.wait_ge(x_turned, c + 1)
                for r in range(3):
                    first_col = (r - c * P) % 3
                    last = nc.vector.tensor_scalar(ids[:, c * P + first_col:(c + 1) * P:3],
                                                   turn_ps[:, first_col:P:3],
                                                   field_base[:, r:r + 1], None, ALU.add)
                last.then_inc(ids_ready, 1)
            nc.vector.memset(eT[:, :, :, F:Q], 0.0).then_inc(zeroed, 1)
            nc.vector.memset(attT[:, :, :, F:Q], 0.0).then_inc(zeroed, 1)
            nc.vector.memset(probs[:, :, :, F:Q], 0.0).then_inc(zeroed, 1)
            nc.vector.memset(mark_w[:, :, F:Q], 0.0).then_inc(zeroed, 1)
            dve.wait_ge(zeroed, N_ZEROED)

            def low_m(lay):
                dve.wait_ge(m_high, lay + 1)
                nc.vector.tensor_tensor(mT_low[:, lay, :, :], m_ps[lay], mT_high[:, lay, :, :],
                                        ALU.subtract).then_inc(m_copied, 1)

            low_m(0)
            slot(0, 0, first=True)
            low_m(1)
            low_m(2)
            dve.wait_ge(m_high, L + 1)
            for c in range(1, JOBS):
                slot(0, c, first=True)
            dve.wait_ge(tail_loaded, N_TAIL_LOADED)
            for c in range(P // HID):
                p = slice(c * HID, (c + 1) * HID)
                last = nc.vector.tensor_copy(w3_blocks[p, p], w3_col[p, :].to_broadcast([HID, HID]))
            last.then_inc(w3_done, 1)
            with dve.Fori(1, LAST) as i:
                for c in range(JOBS):
                    slot(i, c)
            for c in range(JOBS + 1):
                slot(LAST, c, drain=(c >= JOBS), last_it=True)
            last_marks()
            dve.wait_ge(att_summed, 1)
            dve.wait_ge(sig_done, 1)
            nc.vector.tensor_tensor(logit[:], out_ps[:, :], dnn[:], ALU.add).then_inc(logit_done, 1)


_INS = ['r_x', 'L0_rec_emb_table', 'L0_rec_Wq', 'L0_rec_Wk', 'L0_rec_Wv', 'L0_rec_final_w', 'L0_rec_W1',
        'L0_rec_b1', 'L0_rec_W2', 'L0_rec_b2', 'L0_rec_W3', 'L0_rec_b3']


def _constants(np):
    P, HID, F, DIM = 128, 32, 24, 1000
    ident = np.eye(P, dtype=np.float32)
    fold = np.tile(np.eye(HID, dtype=np.float32), (P // HID, 1))
    p = np.arange(P)
    base = np.stack([((P * n + p) % F) * DIM for n in range(3)], axis=1).astype(np.float32)
    quads = np.repeat(np.repeat(np.eye(P // HID, dtype=np.float32), HID, axis=0), HID, axis=1)
    return np.ascontiguousarray(np.concatenate([ident, fold, base, quads], axis=1))


def kernel(**inputs):
    import numpy as _np
    import concourse.bacc as _bacc
    from concourse import mybir as _mybir
    from concourse.bass_utils import run_bass_kernel_spmd as _run

    nc = _bacc.Bacc("TRN2", target_bir_lowering=False, num_devices=1)
    arrays, args = {}, []
    for name in _INS:
        a = _np.ascontiguousarray(inputs[name])
        arrays[f"in_{name}_dram"] = a
        args.append(nc.dram_tensor(f"in_{name}_dram", a.shape, _mybir.dt.from_np(a.dtype), kind="ExternalInput").ap())
    consts = _constants(_np)
    arrays["consts_dram"] = consts
    args.append(nc.dram_tensor("consts_dram", consts.shape, _mybir.dt.float32, kind="ExternalInput").ap())
    args.append(nc.dram_tensor("out_0_dram", (2048, 1), _mybir.dt.float32, kind="ExternalOutput").ap())
    attention_recommender_kernel(nc, *args)
    r = _run(nc, [arrays], core_ids=[0])
    return r.results[0]["out_0_dram"]
```
